# Optimizing a Trainium2 kernel written in Bass

```python
import numpy as np
import jax
import jax.numpy as jnp

def _softmax(x, axis=-1):
    return jax.nn.softmax(x, axis=axis)

def _gelu(x):
    return jax.nn.gelu(x, approximate=True)

def _silu(x):
    return jax.nn.silu(x)

def _sigmoid(x):
    return jax.nn.sigmoid(x)

def _layernorm(x, axis=-1, eps=1e-05):
    m = jnp.mean(x, axis=axis, keepdims=True)
    v = jnp.var(x, axis=axis, keepdims=True)
    return (x - m) / jnp.sqrt(v + eps)

def _scatter_add(tgt, idx, src, axis=0):
    return tgt.at[idx].add(src)

def _segment_sum(src, seg, n):
    return jax.ops.segment_sum(src, seg, n)
kernel_name = 'mk_decoder_preln_d1_seqx_r2_efd7c8'

def setup_inputs(seed: int=0):
    np.random.seed(seed)
    _w = jnp.asarray

    def _rec_inputs():
        import jax
        import jax.numpy as jnp
        _rk = jax.random.key(seed)
        x = -0.0005207 + 1.001 * jax.random.normal(jax.random.fold_in(_rk, 1), (4, 1024, 512), jnp.float32)
        _lenS = 1024 - jax.random.randint(jax.random.fold_in(_rk, 7), (4,), 0, max(1, 1024 // 4) + 1, jnp.int32)
        _lenS2 = 1024 - jax.random.randint(jax.random.fold_in(_rk, 8), (4,), 0, max(1, 1024 // 4) + 1, jnp.int32)
        _ctx_1024P = jax.random.normal(jax.random.fold_in(_rk, 11), (4, 16, 512), jnp.float32)
        _ctx_1024c = jax.random.dirichlet(jax.random.fold_in(_rk, 511), 0.3 * jnp.ones((16,), jnp.float32), (4, 1024))
        _ctx_1024t = jnp.einsum('bsk,bkd->bsd', _ctx_1024c, _ctx_1024P)
        _ctx_1024t = _ctx_1024t * jax.lax.rsqrt(jnp.mean(jnp.square(_ctx_1024t)) + 1e-12) * 0.953939
        ctx_1024 = -0.000514642 + 1.00011 * (_ctx_1024t + 0.3 * jax.random.normal(jax.random.fold_in(_rk, 611), (4, 1024, 512), jnp.float32))
        return (x, ctx_1024)
    x, ctx_1024 = _rec_inputs()

    def _L0_attn_setup():
        import jax, jax.numpy as jnp
        import numpy as np
        NUM_HEAD = 16
        SCALE = 8.0
        LN_EPS = 1e-05
        key = jax.random.key(seed)
        ks = jax.random.split(key, 9)
        B, S, D = (4, 1024, 512)
        s = 1.0 / np.sqrt(D)
        return {'x': jax.random.normal(ks[0], (B, S, D), dtype=jnp.float32), 'Wq': jax.random.normal(ks[1], (D, D), dtype=jnp.float32) * s, 'bq': jax.random.normal(ks[2], (D,), dtype=jnp.float32) * 0.01, 'Wk': jax.random.normal(ks[3], (D, D), dtype=jnp.float32) * s, 'bk': jax.random.normal(ks[4], (D,), dtype=jnp.float32) * 0.01, 'Wv': jax.random.normal(ks[5], (D, D), dtype=jnp.float32) * s, 'bv': jax.random.normal(ks[6], (D,), dtype=jnp.float32) * 0.01, 'Wf': jax.random.normal(ks[7], (D, D), dtype=jnp.float32) * s, 'bf': jax.random.normal(ks[8], (D,), dtype=jnp.float32) * 0.01}
    _L0_attn_all = _L0_attn_setup()
    _L0_attn_in = {k: v for k, v in _L0_attn_all.items() if k in ('Wq', 'bq', 'Wk', 'bk', 'Wv', 'bv', 'Wf', 'bf')}
    del _L0_attn_all

    def _L0_xattn_setup():
        import jax, jax.numpy as jnp
        import numpy as np
        B, S, NDIMS, NHEADS, NPOS = (1, 1024, 512, 16, 64)
        PER_HEAD = NDIMS // NHEADS

        def cope(query, attn_logits, pos_emb):
            npos_max = pos_emb.shape[-1]
            gates = jax.nn.sigmoid(attn_logits)
            pos = jnp.flip(jnp.cumsum(jnp.flip(gates, axis=-1), axis=-1), axis=-1)
            pos = jnp.minimum(pos, npos_max - 1)
            pos_ceil = jnp.ceil(pos).astype(jnp.int32)
            pos_floor = jnp.floor(pos).astype(jnp.int32)
            logits_int = jnp.einsum('bhqd,dn->bhqn', query, pos_emb)
            logits_ceil = jnp.take_along_axis(logits_int, pos_ceil, axis=-1)
            logits_floor = jnp.take_along_axis(logits_int, pos_floor, axis=-1)
            w = pos - pos_floor
            return logits_ceil * w + logits_floor * (1.0 - w)
        key = jax.random.key(seed)
        ks = jax.random.split(key, 9)
        sc = 1.0 / np.sqrt(NDIMS)
        inp = {'q': jax.random.normal(ks[0], (B, S, NDIMS), jnp.float32), 'k': jax.random.normal(ks[1], (B, S, NDIMS), jnp.float32), 'v': jax.random.normal(ks[2], (B, S, NDIMS), jnp.float32), 'Wq_w': jax.random.normal(ks[3], (NDIMS, NDIMS), jnp.float32) * sc, 'Wq_b': jnp.zeros((NDIMS,), jnp.float32), 'Wk_w': jax.random.normal(ks[4], (NDIMS, NDIMS), jnp.float32) * sc, 'Wk_b': jnp.zeros((NDIMS,), jnp.float32), 'Wv_w': jax.random.normal(ks[5], (NDIMS, NDIMS), jnp.float32) * sc, 'Wv_b': jnp.zeros((NDIMS,), jnp.float32), 'Wo_w': jax.random.normal(ks[6], (NDIMS, NDIMS), jnp.float32) * sc, 'Wo_b': jnp.zeros((NDIMS,), jnp.float32), 'pos_emb': jax.random.normal(ks[7], (PER_HEAD, NPOS), jnp.float32) * 0.02, 'nheads': NHEADS}
        return inp
    _L0_xattn_all = _L0_xattn_setup()
    _L0_xattn_in = {k: v for k, v in _L0_xattn_all.items() if k in ('Wq_w', 'Wq_b', 'Wk_w', 'Wk_b', 'Wv_w', 'Wv_b', 'Wo_w', 'Wo_b', 'pos_emb')}
    del _L0_xattn_all

    def _L0_ffn_setup():
        import jax, jax.numpy as jnp
        import numpy as np
        B, S, D, H, E = (64, 512, 512, 64, 8)
        EPS = 1e-05
        key = jax.random.key(seed)
        ks = jax.random.split(key, 8)
        x = jax.random.normal(ks[0], (B, S, D), jnp.float32)
        return {'x': x, 'ln_g': jnp.ones((D,), jnp.float32), 'ln_b': jnp.zeros((D,), jnp.float32), 'bn_g': jnp.ones((D,), jnp.float32), 'bn_b': jnp.zeros((D,), jnp.float32), 'bn_mean': jax.random.normal(ks[1], (D,), jnp.float32) * 0.01, 'bn_var': jnp.ones((D,), jnp.float32), 'Wr': jax.random.normal(ks[2], (D, E), jnp.float32) * 0.02, 'br': jnp.zeros((E,), jnp.float32), 'W_down': jax.random.normal(ks[3], (E, D, H), jnp.float32) * 0.02, 'b_down': jnp.zeros((E, H), jnp.float32), 'W_up': jax.random.normal(ks[4], (E, H, D), jnp.float32) * 0.02, 'b_up': jnp.zeros((E, D), jnp.float32)}
    _L0_ffn_all = _L0_ffn_setup()
    _L0_ffn_in = {k: v for k, v in _L0_ffn_all.items() if k in ('ln_g', 'ln_b', 'bn_g', 'bn_b', 'bn_mean', 'bn_var', 'Wr', 'br', 'W_down', 'b_down', 'W_up', 'b_up')}
    del _L0_ffn_all
    return {'x': x, 'ctx_1024': ctx_1024, 'L0_attn_Wq': _L0_attn_in['Wq'], 'L0_attn_bq': _L0_attn_in['bq'], 'L0_attn_Wk': _L0_attn_in['Wk'], 'L0_attn_bk': _L0_attn_in['bk'], 'L0_attn_Wv': _L0_attn_in['Wv'], 'L0_attn_bv': _L0_attn_in['bv'], 'L0_attn_Wf': _L0_attn_in['Wf'], 'L0_attn_bf': _L0_attn_in['bf'], 'L0_xattn_Wq_w': _L0_xattn_in['Wq_w'], 'L0_xattn_Wq_b': _L0_xattn_in['Wq_b'], 'L0_xattn_Wk_w': _L0_xattn_in['Wk_w'], 'L0_xattn_Wk_b': _L0_xattn_in['Wk_b'], 'L0_xattn_Wv_w': _L0_xattn_in['Wv_w'], 'L0_xattn_Wv_b': _L0_xattn_in['Wv_b'], 'L0_xattn_Wo_w': _L0_xattn_in['Wo_w'], 'L0_xattn_Wo_b': _L0_xattn_in['Wo_b'], 'L0_xattn_pos_emb': _L0_xattn_in['pos_emb'], 'L0_ffn_ln_g': _L0_ffn_in['ln_g'], 'L0_ffn_ln_b': _L0_ffn_in['ln_b'], 'L0_ffn_bn_g': _L0_ffn_in['bn_g'], 'L0_ffn_bn_b': _L0_ffn_in['bn_b'], 'L0_ffn_bn_mean': _L0_ffn_in['bn_mean'], 'L0_ffn_bn_var': _L0_ffn_in['bn_var'], 'L0_ffn_Wr': _L0_ffn_in['Wr'], 'L0_ffn_br': _L0_ffn_in['br'], 'L0_ffn_W_down': _L0_ffn_in['W_down'], 'L0_ffn_b_down': _L0_ffn_in['b_down'], 'L0_ffn_W_up': _L0_ffn_in['W_up'], 'L0_ffn_b_up': _L0_ffn_in['b_up']}

def reference(x, ctx_1024, L0_attn_Wq, L0_attn_bq, L0_attn_Wk, L0_attn_bk, L0_attn_Wv, L0_attn_bv, L0_attn_Wf, L0_attn_bf, L0_xattn_Wq_w, L0_xattn_Wq_b, L0_xattn_Wk_w, L0_xattn_Wk_b, L0_xattn_Wv_w, L0_xattn_Wv_b, L0_xattn_Wo_w, L0_xattn_Wo_b, L0_xattn_pos_emb, L0_ffn_ln_g, L0_ffn_ln_b, L0_ffn_bn_g, L0_ffn_bn_b, L0_ffn_bn_mean, L0_ffn_bn_var, L0_ffn_Wr, L0_ffn_br, L0_ffn_W_down, L0_ffn_b_down, L0_ffn_W_up, L0_ffn_b_up):
    import jax
    import jax.numpy as jnp

    def _L0_attn_ref(x, Wq, bq, Wk, bk, Wv, bv, Wf, bf):
        import jax, jax.numpy as jnp
        import numpy as np
        NUM_HEAD = 16
        SCALE = 8.0
        LN_EPS = 1e-05
        B, S, D = x.shape
        d = D // NUM_HEAD
        q = x @ Wq + bq
        k = x @ Wk + bk
        v = x @ Wv + bv
        q = q.reshape(B * NUM_HEAD, -1, d)
        k = k.reshape(B * NUM_HEAD, -1, d)
        v = v.reshape(B * NUM_HEAD, -1, d)
        attn = jax.nn.softmax(jnp.einsum('bqd,bkd->bqk', q, k) * SCALE, axis=-1)
        ctx = jnp.einsum('bqk,bkd->bqd', attn, v).reshape(B, S, D)
        ctx = ctx + x
        mu = jnp.mean(ctx, axis=-1, keepdims=True)
        var = jnp.var(ctx, axis=-1, keepdims=True)
        ctx = (ctx - mu) * jax.lax.rsqrt(var + LN_EPS)
        return ctx @ Wf + bf

    def _L0_xattn_ref(q, k, v, Wq_w, Wq_b, Wk_w, Wk_b, Wv_w, Wv_b, Wo_w, Wo_b, pos_emb, nheads):
        import jax, jax.numpy as jnp
        import numpy as np
        B, S, NDIMS, NHEADS, NPOS = (1, 1024, 512, 16, 64)
        PER_HEAD = NDIMS // NHEADS

        def cope(query, attn_logits, pos_emb):
            npos_max = pos_emb.shape[-1]
            gates = jax.nn.sigmoid(attn_logits)
            pos = jnp.flip(jnp.cumsum(jnp.flip(gates, axis=-1), axis=-1), axis=-1)
            pos = jnp.minimum(pos, npos_max - 1)
            pos_ceil = jnp.ceil(pos).astype(jnp.int32)
            pos_floor = jnp.floor(pos).astype(jnp.int32)
            logits_int = jnp.einsum('bhqd,dn->bhqn', query, pos_emb)
            logits_ceil = jnp.take_along_axis(logits_int, pos_ceil, axis=-1)
            logits_floor = jnp.take_along_axis(logits_int, pos_floor, axis=-1)
            w = pos - pos_floor
            return logits_ceil * w + logits_floor * (1.0 - w)
        b, s, ndims = q.shape
        d = ndims // nheads

        def heads(x, W, bb):
            y = x @ W.T + bb
            return y.reshape(b, s, nheads, d).transpose(0, 2, 1, 3)
        Q = heads(q, Wq_w, Wq_b)
        K = heads(k, Wk_w, Wk_b)
        V = heads(v, Wv_w, Wv_b)
        logits = jnp.einsum('bhqd,bhkd->bhqk', Q, K) / jnp.sqrt(jnp.asarray(d, Q.dtype))
        scores = jax.nn.softmax(logits + cope(Q, logits, pos_emb), axis=-1)
        out = jnp.einsum('bhqk,bhkd->bhqd', scores, V)
        out = out.transpose(0, 2, 1, 3).reshape(b, s, ndims)
        return out @ Wo_w.T + Wo_b

    def _L0_ffn_ref(x, ln_g, ln_b, bn_g, bn_b, bn_mean, bn_var, Wr, br, W_down, b_down, W_up, b_up):
        import jax, jax.numpy as jnp
        import numpy as np
        B, S, D, H, E = (64, 512, 512, 64, 8)
        EPS = 1e-05
        mu = jnp.mean(x, axis=-1, keepdims=True)
        var = jnp.var(x, axis=-1, keepdims=True)
        z = (x - mu) * jax.lax.rsqrt(var + EPS) * ln_g + ln_b
        z_sent = jnp.mean(z, axis=1)
        z_bn = (z_sent - bn_mean) * jax.lax.rsqrt(bn_var + EPS) * bn_g + bn_b
        probs = jax.nn.softmax(z_bn @ Wr + br, axis=-1)
        idx = jnp.argmax(probs, axis=-1)
        gate = jnp.take_along_axis(probs, idx[:, None], axis=1)[:, 0]
        h = jax.nn.relu(jnp.einsum('bsd,bdh->bsh', z, W_down[idx]) + b_down[idx][:, None, :])
        y = jnp.einsum('bsh,bhd->bsd', h, W_up[idx]) + b_up[idx][:, None, :]
        return y * gate[:, None, None]
    x = x + _L0_attn_ref(_layernorm(x, axis=-1), L0_attn_Wq, L0_attn_bq, L0_attn_Wk, L0_attn_bk, L0_attn_Wv, L0_attn_bv, L0_attn_Wf, L0_attn_bf)
    x = x + _L0_xattn_ref(_layernorm(x, axis=-1), ctx_1024, ctx_1024, L0_xattn_Wq_w, L0_xattn_Wq_b, L0_xattn_Wk_w, L0_xattn_Wk_b, L0_xattn_Wv_w, L0_xattn_Wv_b, L0_xattn_Wo_w, L0_xattn_Wo_b, L0_xattn_pos_emb, 16)
    x = x + _L0_ffn_ref(_layernorm(x, axis=-1), L0_ffn_ln_g, L0_ffn_ln_b, L0_ffn_bn_g, L0_ffn_bn_b, L0_ffn_bn_mean, L0_ffn_bn_var, L0_ffn_Wr, L0_ffn_br, L0_ffn_W_down, L0_ffn_b_down, L0_ffn_W_up, L0_ffn_b_up)
    return x

_drawn_inputs = setup_inputs


def setup_inputs(seed=0):
    import zlib

    import numpy as np

    out = dict(_drawn_inputs(seed))
    spreads = {'L0_xattn_Wq_b': (0.0, 0.565),
     'L0_xattn_Wk_b': (0.0, 2.0),
     'L0_xattn_Wv_b': (0.0, 0.1),
     'L0_xattn_Wo_b': (0.0, 0.1),
     'L0_ffn_ln_g': (1.0, 0.6),
     'L0_ffn_ln_b': (0.0, 0.8),
     'L0_ffn_bn_g': (1.0, 0.6),
     'L0_ffn_bn_b': (0.0, 0.8),
     'L0_ffn_bn_var': (1.0, 0.6),
     'L0_ffn_br': (0.0, 0.8),
     'L0_ffn_b_down': (0.0, 0.8),
     'L0_ffn_b_up': (0.0, 0.679)}
    factors = {'L0_attn_bv': 8.0,
     'L0_attn_bf': 8.0,
     'L0_xattn_pos_emb': 8.0,
     'L0_ffn_bn_mean': 8.0,
     'L0_ffn_Wr': 4.872,
     'L0_ffn_W_down': 8.0,
     'L0_ffn_W_up': 8.0}
    for name, (base, spread) in spreads.items():
        noise = np.random.default_rng([zlib.crc32(name.encode()), seed]).standard_normal(out[name].shape)
        drawn = base * np.exp(spread * noise) if base else spread * noise
        out[name] = jnp.asarray(drawn.astype(out[name].dtype))
    for name, factor in factors.items():
        out[name] = (out[name] * factor).astype(out[name].dtype)
    return out
```

```python
from contextlib import ExitStack

import concourse.bass as bass
from concourse import mybir

F32 = mybir.dt.float32
U32 = mybir.dt.uint32
ALU = mybir.AluOpType
ACT = mybir.ActivationFunctionType
AX = mybir.AxisListType

B, SEQ, D = 4, 1024, 512
ROWS = B * SEQ
ROW_TILES = ROWS // 128
KT = D // 128
HEADS, DH = 16, 32
A_HEADS = B * HEADS
A_SCALE = 8.0
E, H = 8, 64
N_LOADS = 15
EPS = 1e-5
D_HEAD = DH
NPOS = 64
QT = 128
LEVELS = [32, 16, 8, 4, 2, 1]
NL = len(LEVELS)
PAD = 96
SCALE = 1.0 / float(DH) ** 0.5

def allocators(nc, ctx):
    sems = []

    def sb(name, shape, dt=F32):
        return ctx.enter_context(nc.sbuf_tensor(name, shape, dt))

    def ps(name, shape, dt=F32):
        return ctx.enter_context(nc.psum_tensor(name, shape, dt))

    def sem(name, at_first=0):
        sems.append((ctx.enter_context(nc.semaphore(name)), at_first))
        return sems[-1][0]

    return sb, ps, sem, sems


def open_block(nc, ctx, sems):
    def clear():
        for s, _ in sems:
            nc.gpsimd.sem_clear(s)
        nc.all_engine_barrier()

    for s, at_first in sems:
        if at_first:
            nc.gpsimd.sem_inc(s, at_first)
    nc.all_engine_barrier()
    ctx.callback(clear)
    return ctx.enter_context(nc.Block())


def slots(sem, name, at_first=1):
    return [sem(f"{name}{x}", at_first) for x in range(2)]


def dma_slots(sem, name):
    return slots(sem, name, 16)


def norm_buffers(sb, sem, name):
    t = {n: [sb(f"{name}_{n}{x}", [128, m]) for x in range(2)] for n, m in (("stats", 6), ("mv", 2), ("std", 1), ("rstd", 1))}
    for n in ("s_stats", "s_mv", "s_var", "s_std", "s_rstd"):
        t[n] = slots(sem, f"{name}_{n}")
    t["s_held"] = sem(f"{name}_held")
    return t


def norm_measure(nc, dve, t, x, j, rows):
    nc.vector.bn_stats(t["stats"][x][:, :], rows).then_inc(t["s_stats"][x], 1)
    dve.wait_ge(t["s_stats"][x], j + 2)
    dve.sem_inc(t["s_held"], 1)
    nc.vector.bn_aggr(t["mv"][x][:, :], t["stats"][x][:, :]).then_inc(t["s_mv"][x], 1)
    dve.wait_ge(t["s_mv"][x], j + 2)
    nc.vector.tensor_scalar(t["mv"][x][:, 1:2], t["mv"][x][:, 1:2], EPS, None, ALU.add).then_inc(t["s_var"][x], 1)


def norm_root(nc, act, t, x, j):
    act.wait_ge(t["s_var"][x], j + 2)
    nc.scalar.activation(t["std"][x][:, :], t["mv"][x][:, 1:2], ACT.Sqrt).then_inc(t["s_std"][x], 1)


def norm_scale(nc, dve, t, x, j, out, rows):
    dve.wait_ge(t["s_std"][x], j + 2)
    nc.vector.reciprocal(t["rstd"][x][:, :], t["std"][x][:, :]).then_inc(t["s_rstd"][x], 1)
    dve.wait_ge(t["s_rstd"][x], j + 2)
    return nc.vector.tensor_scalar(out, rows, t["mv"][x][:, 0:1], t["rstd"][x][:, 0:1], ALU.subtract, ALU.mult)


def build_memory_projections(nc, ctx_t, wk_t, bk, wv_t, bv, k_heads, v_heads):
    with ExitStack() as ctx:
        sb, ps, sem, sems = allocators(nc, ctx)
        wk, wv = (sb(f"m_w{n}", [128, KT, D]) for n in "kv")
        bk_row, bv_row = (sb(f"m_b{n}", [1, D]) for n in "kv")
        ones = sb("m_ones", [1, 512])
        tokens = sb("m_tokens", [128, KT, SEQ])
        out_sb = [sb(f"m_out{n}", [128, 512]) for n in range(4)]
        acc = [ps(f"m_acc{n}", [128, 512]) for n in range(4)]
        s_w, s_ones, s_tokens, s_used = sem("m_w"), sem("m_ones"), sem("m_tokens"), sem("m_used", 1)
        s_acc = [sem(f"m_acc{n}") for n in range(4)]
        s_sb = [sem(f"m_sb{n}", 1) for n in range(4)]
        s_out = [sem(f"m_outs{n}", 16) for n in range(4)]
        block = open_block(nc, ctx, sems)
        GROUPS = 16

        @block.sync
        def _(sp):
            for dst, src in ((wk, wk_t), (wv, wv_t)):
                sp.dma_start(dst[:, :, :], src.rearrange("(k p) n -> p k n", p=128)).then_inc(s_w, 16)
            for dst, src in ((bk_row, bk), (bv_row, bv)):
                sp.dma_start(dst[:, :], src.rearrange("(a n) -> a n", a=1)).then_inc(s_w, 16)
            with sp.Fori(0, B) as b:
                sp.wait_ge(s_used, b + 1)
                sp.dma_start(tokens[:, :, :], ctx_t[bass.ds(b, 1)].rearrange("a (k p) t -> (a p) k t", p=128))\
                    .then_inc(s_tokens, 16)
                for g in range(GROUPS):
                    n = g % 4
                    sp.wait_ge(s_sb[n], 4 * b + g // 4 + 2)
                    if g < 8:
                        f, half = g // 2, g % 2
                        dst = k_heads[bass.ds(b, 1), f * 128:(f + 1) * 128, half * 512:(half + 1) * 512]
                        sp.dma_start(dst.rearrange("a p t -> (a p) t"), out_sb[n][:, :]).then_inc(s_out[n], 16)
                    else:
                        dst = v_heads[bass.ds(b * HEADS, HEADS), :, g - 8, :]
                        sp.dma_start(dst.rearrange("h p d -> p h d"),
                                     out_sb[n][:, :].rearrange("p (h d) -> p h d", h=HEADS)).then_inc(s_out[n], 16)
            for n in range(4):
                sp.wait_ge(s_out[n], 16 * (4 * B + 1))

        @block.tensor
        def _(pe):
            pe.wait_ge(s_w, 64)
            pe.wait_ge(s_ones, 1)
            with pe.Fori(0, B) as b:
                pe.wait_ge(s_tokens, 16 * (b + 1))
                for g in range(GROUPS):
                    n = g % 4
                    pe.wait_ge(s_sb[n], 4 * b + g // 4 + 1)
                    for k in range(KT):
                        if g < 8:
                            f, half = g // 2, g % 2
                            nc.tensor.matmul(acc[n][:, :], wk[:, k, f * 128:(f + 1) * 128],
                                             tokens[:, k, half * 512:(half + 1) * 512], start=(k == 0), stop=False)
                        else:
                            c = g - 8
                            nc.tensor.matmul(acc[n][:, :], tokens[:, k, c * 128:(c + 1) * 128], wv[:, k, :],
                                             start=(k == 0), stop=False)
                    if g < 8:
                        mm = nc.tensor.matmul(acc[n][:, :], bk_row[:, f * 128:(f + 1) * 128], ones[:, :],
                                              start=False, stop=True)
                    else:
                        mm = nc.tensor.matmul(acc[n][:, :], ones[:, 0:128], bv_row[:, :], start=False, stop=True)
                    mm.then_inc(s_acc[n], 1)
                pe.wait_ge(s_acc[(GROUPS - 1) % 4], 4 * (b + 1))
                pe.sem_inc(s_used, 1)

        def drain(eng, copy, mine):
            with eng.Fori(0, B) as b:
                for g in mine:
                    n = g % 4
                    eng.wait_ge(s_acc[n], 4 * b + g // 4 + 1)
                    eng.wait_ge(s_out[n], 16 * (4 * b + g // 4 + 1))
                    copy(out_sb[n][:, :], acc[n][:, :]).then_inc(s_sb[n], 1)

        @block.vector
        def _(dve):
            nc.vector.memset(ones[:, :], 1.0).then_inc(s_ones, 1)
            drain(dve, nc.vector.tensor_copy, range(0, GROUPS, 2))

        @block.scalar
        def _(act):
            drain(act, nc.scalar.copy, range(1, GROUPS, 2))

        @block.gpsimd
        def _(pool):
            pass


def row_tile(a, j, x):
    return a[bass.ds((2 * j + x) * 128, 128), :]


def build_self_projections(nc, x_rows, wq, bq, wk, bk, wv, bv, xn_rows, q_heads, k_heads, v_heads, ident_dram):
    with ExitStack() as ctx:
        sb, ps, sem, sems = allocators(nc, ctx)
        w = {n: sb(f"s_w{n}", [128, KT, D]) for n in "qkv"}
        brow = {n: sb(f"s_b{n}", [1, D]) for n in "qkv"}
        ones = sb("s_ones", [1, 128])
        ident = sb("s_ident", [128, 128])
        xt, xn, xT = ([sb(f"s_{n}{x}", [128, D]) for x in range(2)] for n in ("xt", "xn", "xT"))
        qk_sb = {n: [sb(f"s_{n}sb{x}", [DH, 2, HEADS, 64]) for x in range(2)] for n in "qk"}
        v_sb = [sb(f"s_vsb{x}", [128, 2, 256]) for x in range(2)]
        turn_ps = [ps(f"s_turn{x}", [128, KT, 128]) for x in range(2)]
        out_ps = {n: [ps(f"s_{n}ps{x}", [128, 512]) for x in range(2)] for n in "qkv"}
        s_w, s_ones = sem("s_wload"), sem("s_ones")
        s_xn, s_turn, s_xT, s_mm, s_evq, s_evk, s_evv = (
            slots(sem, f"s_s{n}") for n in ("xn", "turn", "xT", "mm", "evq", "evk", "evv"))
        s_x, s_xnout, s_outq, s_outk, s_outv = (dma_slots(sem, f"s_s{n}") for n in ("x", "xnout", "outq", "outk", "outv"))
        norm = norm_buffers(sb, sem, "s_n")
        block = open_block(nc, ctx, sems)

        @block.sync
        def _(sp):
            sp.dma_start(ident[:, :], ident_dram).then_inc(s_w, 16)
            for n, a in (("q", wq), ("k", wk), ("v", wv)):
                sp.dma_start(w[n][:, :, :], a.rearrange("(k p) n -> p k n", p=128)).then_inc(s_w, 16)
            for n, a in (("q", bq), ("k", bk), ("v", bv)):
                sp.dma_start(brow[n][:, :], a.rearrange("(a n) -> a n", a=1)).then_inc(s_w, 16)
            with sp.Fori(0, ROW_TILES // 2) as j:
                for x in range(2):
                    sp.wait_ge(s_xn[x], j + 1)
                    sp.dma_start(xt[x][:, :], row_tile(x_rows, j, x)).then_inc(s_x[x], 16)
                for x in range(2):
                    sp.wait_ge(s_xn[x], j + 2)
                    sp.dma_start(row_tile(xn_rows, j, x), xn[x][:, :]).then_inc(s_xnout[x], 16)
                for x in range(2):
                    head = 4 * j + 2 * x
                    for n, dst, s_ev, s_out in (("q", q_heads, s_evq, s_outq), ("k", k_heads, s_evk, s_outk)):
                        sp.wait_ge(s_ev[x], j + 2)
                        sp.dma_start(dst[bass.ds(head, 2)].rearrange("h d t -> d h t"),
                                     qk_sb[n][x][:, :, :, :].rearrange("d h c r -> d h (c r)")).then_inc(s_out[x], 16)
                    sp.wait_ge(s_evv[x], j + 2)
                    sp.dma_start(v_heads[bass.ds(head, 2)].rearrange("h p c d -> p h (c d)"), v_sb[x][:, :, :])\
                        .then_inc(s_outv[x], 16)
            for s in (s_xnout, s_outq, s_outk, s_outv):
                for x in range(2):
                    sp.wait_ge(s[x], 16 * (ROW_TILES // 2 + 1))

        @block.vector
        def _(dve):
            nc.vector.memset(ones[:, :], 1.0).then_inc(s_ones, 1)
            with dve.Fori(0, ROW_TILES // 2) as j:
                for x in range(2):
                    dve.wait_ge(s_x[x], 16 * (j + 2))
                    norm_measure(nc, dve, norm, x, j, xt[x][:, :])
                for x in range(2):
                    dve.wait_ge(s_xnout[x], 16 * (j + 1))
                    dve.wait_ge(s_turn[x], j + 1)
                    norm_scale(nc, dve, norm, x, j, xn[x][:, :], xt[x][:, :]).then_inc(s_xn[x], 1)
                for x in range(2):
                    dve.wait_ge(s_mm[x], j + 2)
                    dve.wait_ge(s_outk[x], 16 * (j + 1))
                    for c4 in range(4):
                        ins = nc.vector.tensor_copy(
                            qk_sb["k"][x][:, :, :, :].rearrange("d h (o c) r -> d o c h r", c=4)[:, :, c4],
                            out_ps["k"][x][c4 * DH:(c4 + 1) * DH, :].rearrange("p (o h r) -> p o h r", h=2, r=64))
                    ins.then_inc(s_evk[x], 1)
                    dve.wait_ge(s_outv[x], 16 * (j + 1))
                    nc.vector.tensor_copy(v_sb[x][:, :, :], out_ps["v"][x][:, :].rearrange("p (h n) -> p h n", h=2))\
                        .then_inc(s_evv[x], 1)

        @block.scalar
        def _(act):
            with act.Fori(0, ROW_TILES // 2) as j:
                for x in range(2):
                    norm_root(nc, act, norm, x, j)
                for x in range(2):
                    act.wait_ge(s_turn[x], j + 2)
                    act.wait_ge(s_mm[x], j + 1)
                    nc.scalar.copy(xT[x][:, :], turn_ps[x][:, :, :].rearrange("p k r -> p (k r)")).then_inc(s_xT[x], 1)
                for x in range(2):
                    act.wait_ge(s_mm[x], j + 2)
                    act.wait_ge(s_outq[x], 16 * (j + 1))
                    for c4 in range(4):
                        ins = nc.scalar.copy(
                            qk_sb["q"][x][:, :, :, :].rearrange("d h (o c) r -> d o c h r", c=4)[:, :, c4],
                            out_ps["q"][x][c4 * DH:(c4 + 1) * DH, :].rearrange("p (o h r) -> p o h r", h=2, r=64))
                    ins.then_inc(s_evq[x], 1)

        @block.tensor
        def _(pe):
            pe.wait_ge(s_w, 16 * 7)
            pe.wait_ge(s_ones, 1)
            with pe.Fori(0, ROW_TILES // 2) as j:
                for x in range(2):
                    pe.wait_ge(s_xn[x], j + 2)
                    pe.wait_ge(s_xT[x], j + 1)
                    for k in range(KT):
                        mm = nc.tensor.transpose(turn_ps[x][:, k, :], xn[x][:, k * 128:(k + 1) * 128], ident[:, :])
                    mm.then_inc(s_turn[x], 1)
                for x in range(2):
                    pe.wait_ge(s_xT[x], j + 2)
                    pe.wait_ge(s_evq[x], j + 1)
                    pe.wait_ge(s_evk[x], j + 1)
                    for n in "qk":
                        for o in range(4):
                            dst = out_ps[n][x][:, o * 128:(o + 1) * 128]
                            for k in range(KT):
                                nc.tensor.matmul(dst, w[n][:, k, o * 128:(o + 1) * 128], xT[x][:, k * 128:(k + 1) * 128],
                                                 start=(k == 0), stop=False)
                            nc.tensor.matmul(dst, brow[n][:, o * 128:(o + 1) * 128], ones[:, :], start=False, stop=True)
                    pe.wait_ge(s_evv[x], j + 1)
                    for h in range(2):
                        for odd in range(2):
                            dst = out_ps["v"][x][odd * 64:(odd + 1) * 64, h * 256:(h + 1) * 256]
                            for k in range(KT):
                                nc.tensor.matmul(dst, xT[x][:, k * 128 + h * 64:k * 128 + (h + 1) * 64],
                                                 w["v"][:, k, odd * 256:(odd + 1) * 256], start=(k == 0), stop=False)
                            mm = nc.tensor.matmul(dst, ones[:, 0:64], brow["v"][:, odd * 256:(odd + 1) * 256],
                                                  start=False, stop=True)
                    mm.then_inc(s_mm[x], 1)

        @block.gpsimd
        def _(pool):
            pass


def build_self_attention(nc, q_heads, k_heads, v_heads, reach, ident_dram):
    with ExitStack() as ctx:
        sb, ps, sem, sems = allocators(nc, ctx)
        ident = sb("a_ident", [128, 128])
        qs = [sb(f"a_q{s}", [DH, 2, QT]) for s in range(2)]
        ks = [sb(f"a_k{s}", [DH, SEQ]) for s in range(2)]
        vs = [sb(f"a_v{s}", [128, 8, DH]) for s in range(2)]
        probs = [sb(f"a_probs{x}", [128, SEQ]) for x in range(2)]
        pt = [sb(f"a_pt{x}", [128, 8, QT]) for x in range(2)]
        rowmax, bias, den, rden = ([sb(f"a_{n}{x}", [128, 1]) for x in range(2)] for n in ("max", "bias", "den", "rden"))
        o_sb = [sb(f"a_o{x}", [128, DH]) for x in range(2)]
        score_ps = [ps(f"a_score{x}", [128, 2, 512]) for x in range(2)]
        pt_ps = ps("a_ptps", [128, 8, QT])
        o_ps = [ps(f"a_ops{x}", [128, 512]) for x in range(2)]
        s_const = sem("a_const")
        s_qk, s_v = slots(sem, "a_qk", 0), slots(sem, "a_vload", 0)
        (s_scored, s_max, s_bias, s_exp, s_turned, s_kept_a, s_kept_d, s_pv, s_rden, s_norm) = (
            sem(f"a_s{n}") for n in ("scored", "max", "bias", "exp", "turned", "kept_a", "kept_d", "pv", "rden", "norm"))
        s_out = dma_slots(sem, "a_out")
        block = open_block(nc, ctx, sems)
        n_pairs = A_HEADS * 4
        last = n_pairs - 1

        def pairs(eng, step):
            step(0, 0)
            with eng.Fori(0, (n_pairs - 2) // 2) as j:
                step(2 * j + 1, 1)
                step(2 * j + 2, 0)
            step(last, 1)

        def early(i, n=1):
            return isinstance(i, int) and i < n

        @block.sync
        def _(sp):
            sp.dma_start(ident[:, :], ident_dram).then_inc(s_const, 16)

            def load(i, s):
                if not early(i, 2):
                    sp.wait_ge(s_scored, 2 * i - 2)
                head = i // 4
                sp.dma_start(qs[s][:, :, :], q_heads[bass.ds(head, 1), :, bass.ds((i % 4) * 2 * QT, 2 * QT)]
                             .rearrange("a d (x q) -> (a d) x q", x=2)).then_inc(s_qk[s], 16)
                sp.dma_start(ks[s][:, :], k_heads[bass.ds(head, 1)].rearrange("a d t -> (a d) t")).then_inc(s_qk[s], 16)
                if not early(i, 2):
                    sp.wait_ge(s_pv, 2 * i - 2)
                sp.dma_start(vs[s][:, :, :], v_heads[bass.ds(head, 1)].rearrange("a p c d -> (a p) c d")).then_inc(s_v[s], 16)

            pairs(sp, load)

        @block.tensor
        def _(pe):
            pe.wait_ge(s_const, 16)

            def scores(i, s, x):
                g = 2 * i + x
                if x == 0:
                    pe.wait_ge(s_qk[s], 32 * (i // 2 + 1))
                if not early(i):
                    pe.wait_ge(s_exp, g - 1)
                for n in range(2):
                    mm = nc.tensor.matmul(score_ps[x][:, n, :], qs[s][:, x, :], ks[s][:, n * 512:(n + 1) * 512],
                                          start=True, stop=True)
                mm.then_inc(s_scored, 1)

            def turn(i, x):
                g = 2 * i + x
                pe.wait_ge(s_exp, g + 1)
                if not early(g):
                    pe.wait_ge(s_kept_a, g)
                    pe.wait_ge(s_kept_d, g)
                for c in range(8):
                    mm = nc.tensor.transpose(pt_ps[:, c, :], probs[x][:, c * 128:(c + 1) * 128], ident[:, :])
                mm.then_inc(s_turned, 1)

            def values(i, s, x):
                g = 2 * i + x
                pe.wait_ge(s_kept_a, g + 1)
                pe.wait_ge(s_kept_d, g + 1)
                if x == 0:
                    pe.wait_ge(s_v[s], 16 * (i // 2 + 1))
                if x or not early(i):
                    pe.wait_ge(s_norm, g if x else g - 1)
                for c in range(8):
                    mm = nc.tensor.matmul(o_ps[x][:, 0:DH], pt[x][:, c, :], vs[s][:, c, :], start=(c == 0), stop=(c == 7))
                mm.then_inc(s_pv, 1)

            def step(i, s):
                first, final = early(i), isinstance(i, int) and i == last
                scores(i, s, 1)
                if not first:
                    values(i - 1, 1 - s, 1)
                turn(i, 0)
                if not final:
                    scores(i + 1, 1 - s, 0)
                values(i, s, 0)
                turn(i, 1)

            scores(0, 0, 0)
            pairs(pe, step)
            values(last, 1, 1)

        @block.vector
        def _(dve):
            def peak(i, x):
                g = 2 * i + x
                dve.wait_ge(s_scored, g + 1)
                nc.vector.tensor_reduce(rowmax[x][:, :], score_ps[x][:, :, :], AX.XY, ALU.max).then_inc(s_max, 1)
                if not early(i):
                    dve.wait_ge(s_exp, g - 1)
                dve.wait_ge(s_max, g + 1)
                nc.vector.tensor_scalar(bias[x][:, :], rowmax[x][:, :], -A_SCALE, None, ALU.mult).then_inc(s_bias, 1)

            def keep(i, x):
                g = 2 * i + x
                dve.wait_ge(s_turned, g + 1)
                if not early(i):
                    dve.wait_ge(s_pv, g - 1)
                nc.vector.tensor_copy(pt[x][:, 0:4, :], pt_ps[:, 0:4, :]).then_inc(s_kept_d, 1)

            def norm(i, x):
                g = 2 * i + x
                dve.wait_ge(s_exp, g + 1)
                if x or not early(i):
                    dve.wait_ge(s_norm, g if x else g - 1)
                nc.vector.reciprocal(rden[x][:, :], den[x][:, :]).then_inc(s_rden, 1)
                dve.wait_ge(s_pv, g + 1)
                dve.wait_ge(s_rden, g + 1)
                dve.wait_ge(s_out[x], 32 * i + 16)
                nc.vector.tensor_scalar(o_sb[x][:, :], o_ps[x][:, 0:DH], rden[x][:, 0:1], None, ALU.mult).then_inc(s_norm, 1)

            def step(i, s):
                first, final = early(i), isinstance(i, int) and i == last
                peak(i, 1)
                keep(i, 0)
                if not first:
                    norm(i - 1, 1)
                if not final:
                    peak(i + 1, 0)
                keep(i, 1)
                norm(i, 0)

            peak(0, 0)
            pairs(dve, step)
            norm(last, 1)

        @block.scalar
        def _(act):
            def expo(i, x):
                g = 2 * i + x
                act.wait_ge(s_bias, g + 1)
                if not early(i):
                    act.wait_ge(s_turned, g - 1)
                    act.wait_ge(s_rden, g - 1)
                nc.scalar.activation(probs[x][:, :], score_ps[x][:, :, :].rearrange("p a b -> p (a b)"), ACT.Exp,
                                     bias=bias[x][:, :], scale=A_SCALE, accum_out=den[x][:, :]).then_inc(s_exp, 1)

            def keep(i, x):
                g = 2 * i + x
                act.wait_ge(s_turned, g + 1)
                if not early(i):
                    act.wait_ge(s_pv, g - 1)
                nc.scalar.copy(pt[x][:, 4:8, :], pt_ps[:, 4:8, :]).then_inc(s_kept_a, 1)

            def send(i, x):
                g = 2 * i + x
                act.wait_ge(s_norm, g + 1)
                for half in range(2):
                    act.dma_start(reach(i, x, half), o_sb[x][half * 64:(half + 1) * 64, :]).then_inc(s_out[x], 16)

            def step(i, s):
                first, final = early(i), isinstance(i, int) and i == last
                expo(i, 1)
                keep(i, 0)
                if not first:
                    send(i - 1, 1)
                if not final:
                    expo(i + 1, 0)
                keep(i, 1)
                send(i, 0)

            expo(0, 0)
            pairs(act, step)
            send(last, 1)
            for x in range(2):
                act.wait_ge(s_out[x], 32 * n_pairs + 16)

        @block.gpsimd
        def _(pool):
            pass


def build_self_output(nc, ctx_rows, xn_rows, x_rows, wf, bf, wq_t, bq, x1_rows, q_heads, ident_dram):
    with ExitStack() as ctx:
        sb, ps, sem, sems = allocators(nc, ctx)
        w_f, w_q = sb("o_wf", [128, KT, D]), sb("o_wq", [128, KT, D])
        bf_row, bq_row = sb("o_bf", [1, D]), sb("o_bq", [1, D])
        ones, ident = sb("o_ones", [1, 128]), sb("o_ident", [128, 128])
        att, xn, xr, cn, cT, x1, x1n, x1T, q_sb = ([sb(f"o_{n}{x}", [128, D]) for x in range(2)] for n in (
            "att", "xn", "xr", "cn", "cT", "x1", "x1n", "x1T", "qsb"))
        turn_ps, f_ps, turn2_ps, q_ps = ([ps(f"o_{n}{x}", [128, KT, 128]) for x in range(2)] for n in ("tps", "fps", "t2ps", "qps"))
        s_w, s_ones = sem("o_w"), sem("o_ones")
        s_sum, s_cn, s_turn, s_cT, s_f, s_x1, s_x1n, s_turn2, s_x1T, s_q, s_qsb = (
            slots(sem, f"o_s{n}") for n in ("sum", "cn", "turn", "cT", "f", "x1", "x1n", "turn2", "x1T", "q", "qsb"))
        s_att, s_xr, s_x1out, s_qout = (dma_slots(sem, f"o_s{n}") for n in ("att", "xr", "x1out", "qout"))
        n1, n2 = norm_buffers(sb, sem, "o_n1"), norm_buffers(sb, sem, "o_n2")
        block = open_block(nc, ctx, sems)

        @block.sync
        def _(sp):
            sp.dma_start(ident[:, :], ident_dram).then_inc(s_w, 16)
            for dst, a in ((w_f, wf), (w_q, wq_t)):
                sp.dma_start(dst[:, :, :], a.rearrange("(k p) n -> p k n", p=128)).then_inc(s_w, 16)
            for dst, a in ((bf_row, bf), (bq_row, bq)):
                sp.dma_start(dst[:, :], a.rearrange("(a n) -> a n", a=1)).then_inc(s_w, 16)
            with sp.Fori(0, ROW_TILES // 2) as j:
                for x in range(2):
                    sp.wait_ge(s_cn[x], j + 1)
                    sp.dma_start(att[x][:, :], row_tile(ctx_rows, j, x)).then_inc(s_att[x], 16)
                    sp.dma_start(xn[x][:, :], row_tile(xn_rows, j, x)).then_inc(s_att[x], 16)
                    sp.wait_ge(s_x1[x], j + 1)
                    sp.dma_start(xr[x][:, :], row_tile(x_rows, j, x)).then_inc(s_xr[x], 16)
                for x in range(2):
                    sp.wait_ge(s_x1[x], j + 2)
                    sp.dma_start(row_tile(x1_rows, j, x), x1[x][:, :]).then_inc(s_x1out[x], 16)
                for x in range(2):
                    sp.wait_ge(s_qsb[x], j + 2)
                    t = 2 * j + x
                    dst = q_heads[bass.ds(t // 8, 1), :, bass.ds((t % 8) * 128, 128)]
                    sp.dma_start(dst.rearrange("a (o p) t -> (a p) o t", p=128),
                                 q_sb[x][:, :].rearrange("p (o t) -> p o t", o=4)).then_inc(s_qout[x], 16)
            for s in (s_x1out, s_qout):
                for x in range(2):
                    sp.wait_ge(s[x], 16 * (ROW_TILES // 2 + 1))

        @block.vector
        def _(dve):
            nc.vector.memset(ones[:, :], 1.0).then_inc(s_ones, 1)
            with dve.Fori(0, ROW_TILES // 2) as j:
                for x in range(2):
                    dve.wait_ge(s_att[x], 32 * (j + 1) + 16)
                    nc.vector.tensor_tensor(att[x][:, :], att[x][:, :], xn[x][:, :], ALU.add).then_inc(s_sum[x], 1)
                    dve.wait_ge(s_sum[x], j + 2)
                    norm_measure(nc, dve, n1, x, j, att[x][:, :])
                for x in range(2):
                    dve.wait_ge(s_turn[x], j + 1)
                    norm_scale(nc, dve, n1, x, j, cn[x][:, :], att[x][:, :]).then_inc(s_cn[x], 1)
                for x in range(2):
                    dve.wait_ge(s_f[x], j + 2)
                    dve.wait_ge(s_xr[x], 16 * (j + 2))
                    dve.wait_ge(s_x1out[x], 16 * (j + 1))
                    nc.vector.tensor_tensor(x1[x][:, :], f_ps[x][:, :, :].rearrange("p k n -> p (k n)"), xr[x][:, :], ALU.add)\
                        .then_inc(s_x1[x], 1)
                    dve.wait_ge(s_x1[x], j + 2)
                    norm_measure(nc, dve, n2, x, j, x1[x][:, :])
                for x in range(2):
                    dve.wait_ge(s_turn2[x], j + 1)
                    norm_scale(nc, dve, n2, x, j, x1n[x][:, :], x1[x][:, :]).then_inc(s_x1n[x], 1)

        @block.scalar
        def _(act):
            with act.Fori(0, ROW_TILES // 2) as j:
                for x in range(2):
                    norm_root(nc, act, n1, x, j)
                for x in range(2):
                    act.wait_ge(s_turn[x], j + 2)
                    act.wait_ge(s_f[x], j + 1)
                    nc.scalar.copy(cT[x][:, :], turn_ps[x][:, :, :].rearrange("p k r -> p (k r)")).then_inc(s_cT[x], 1)
                for x in range(2):
                    norm_root(nc, act, n2, x, j)
                for x in range(2):
                    act.wait_ge(s_turn2[x], j + 2)
                    act.wait_ge(s_q[x], j + 1)
                    nc.scalar.copy(x1T[x][:, :], turn2_ps[x][:, :, :].rearrange("p k r -> p (k r)")).then_inc(s_x1T[x], 1)
                for x in range(2):
                    act.wait_ge(s_q[x], j + 2)
                    act.wait_ge(s_qout[x], 16 * (j + 1))
                    nc.scalar.copy(q_sb[x][:, :], q_ps[x][:, :, :].rearrange("p o t -> p (o t)")).then_inc(s_qsb[x], 1)

        @block.tensor
        def _(pe):
            pe.wait_ge(s_w, 16 * 5)
            pe.wait_ge(s_ones, 1)
            with pe.Fori(0, ROW_TILES // 2) as j:
                for x in range(2):
                    pe.wait_ge(s_cn[x], j + 2)
                    pe.wait_ge(s_cT[x], j + 1)
                    for k in range(KT):
                        mm = nc.tensor.transpose(turn_ps[x][:, k, :], cn[x][:, k * 128:(k + 1) * 128], ident[:, :])
                    mm.then_inc(s_turn[x], 1)
                for x in range(2):
                    pe.wait_ge(s_cT[x], j + 2)
                    pe.wait_ge(s_x1[x], j + 1)
                    dst = f_ps[x][:, :, :].rearrange("p k n -> p (k n)")
                    for k in range(KT):
                        nc.tensor.matmul(dst, cT[x][:, k * 128:(k + 1) * 128], w_f[:, k, :], start=(k == 0), stop=False)
                    nc.tensor.matmul(dst, ones[:, :], bf_row[:, :], start=False, stop=True).then_inc(s_f[x], 1)
                for x in range(2):
                    pe.wait_ge(s_x1n[x], j + 2)
                    pe.wait_ge(s_x1T[x], j + 1)
                    for k in range(KT):
                        mm = nc.tensor.transpose(turn2_ps[x][:, k, :], x1n[x][:, k * 128:(k + 1) * 128], ident[:, :])
                    mm.then_inc(s_turn2[x], 1)
                for x in range(2):
                    pe.wait_ge(s_x1T[x], j + 2)
                    pe.wait_ge(s_qsb[x], j + 1)
                    for o in range(4):
                        for k in range(KT):
                            nc.tensor.matmul(q_ps[x][:, o, :], w_q[:, k, o * 128:(o + 1) * 128], x1T[x][:, k * 128:(k + 1) * 128],
                                             start=(k == 0), stop=False)
                        mm = nc.tensor.matmul(q_ps[x][:, o, :], bq_row[:, o * 128:(o + 1) * 128], ones[:, :],
                                              start=False, stop=True)
                    mm.then_inc(s_q[x], 1)

        @block.gpsimd
        def _(pool):
            pass


def build_cope_attention(nc, n_pairs, q_heads, k_heads, v_heads, pos_emb, reach, ident_dram):
    with ExitStack() as ctx:
        sb, ps, sem, sems = allocators(nc, ctx)
        ident = sb("c_ident", [128, 128])
        emb = sb("c_emb", [D_HEAD, NPOS])
        qs = [sb(f"c_q{s}", [D_HEAD, 2, QT]) for s in range(2)]
        ks = [sb(f"c_k{s}", [D_HEAD, SEQ]) for s in range(2)]
        vs = [sb(f"c_v{s}", [128, 8, D_HEAD]) for s in range(2)]
        table = [sb(f"c_table{x}", [128, PAD]) for x in range(2)]
        gate2 = [sb(f"c_gate{x}", [128, SEQ]) for x in range(2)]
        pos = [sb(f"c_pos{x}", [128, SEQ]) for x in range(2)]
        logit = [[sb(f"c_logit{s}{x}", [128, SEQ]) for x in range(2)] for s in range(2)]
        win = [[sb(f"c_win{x}{n}", [128, 2 * SEQ]) for n in range(3)] for x in range(2)]
        base = [[sb(f"c_base{x}{l}", [128, SEQ // b]) for l, b in enumerate(LEVELS)] for x in range(2)]
        interp = [sb(f"c_interp{x}", [128, SEQ]) for x in range(2)]
        pt = sb("c_pt", [128, 8, QT])
        ones = sb("c_ones", [128, 1])
        rowmax = [sb(f"c_max{x}", [128, 1]) for x in range(2)]
        negmax = [sb(f"c_neg{x}", [128, 1]) for x in range(2)]
        den = [sb(f"c_den{x}", [128, 1]) for x in range(2)]
        rden = [sb(f"c_rden{x}", [128, 1]) for x in range(2)]
        o_sb = [sb(f"c_o{x}", [128, D_HEAD]) for x in range(2)]

        score_ps = ps("c_score_ps", [128, 2, 512])
        table_ps = ps("c_table_ps", [128, 512])
        o_ps = ps("c_o_ps", [128, 512])
        mask_ps = ps("c_mask_ps", [128, SEQ])
        pt_ps = ps("c_pt_ps", [128, 8, QT])

        s_const = sem("c_const")
        s_qk = slots(sem, "c_qk", 0)
        s_v = slots(sem, "c_v", 0)
        s_scored = sem("c_scored")
        s_tabled = sem("c_tabled")
        s_taken = sem("c_taken")
        s_scan = sem("c_scan")
        s_copy = sem("c_copy")
        s_pick = sem("c_pick")
        s_leaf = sem("c_leaf")
        s_w = sem("c_w")
        s_pool = sem("c_pool")
        s_read = sem("c_read")
        s_cope = sem("c_cope")
        s_z = sem("c_z")
        s_neg = sem("c_neg")
        s_exp = slots(sem, "c_exp")
        s_rden = slots(sem, "c_rden")
        s_turned = sem("c_turned")
        s_ptcopy = sem("c_ptcopy", 1)
        s_pv = sem("c_pv", 1)
        s_norm = slots(sem, "c_norm")
        s_out = dma_slots(sem, "c_out")
        s_pos, s_mask, s_base, s_base1, s_pick1, s_mask2 = (
            slots(sem, f"c_{n}", 0) for n in ("pos", "mask", "base", "base1", "pick1", "mask2"))
        s_pad = sem("c_pad")
        s_held = sem("c_held")

        block = open_block(nc, ctx, sems)
        last = n_pairs - 1

        def pairs(eng, step, before=None, after=None):
            step(0, 0)
            with eng.Fori(0, (n_pairs - 2) // 2) as j:
                step(2 * j + 1, 1)
                step(2 * j + 2, 0)
            step(last, 1)

        def early(i, n=1):
            return isinstance(i, int) and i < n

        def bits(mask):
            return mask.bitcast(U32)

        def window(l, x):
            b = LEVELS[l]
            w = win[x][2] if l == NL - 1 else win[x][l % 2]
            return w[:, :].rearrange("p (j e) -> p j e", e=2 * b)

        @block.sync
        def _(sp):
            sp.dma_start(ident[:, :], ident_dram).then_inc(s_const, 16)
            sp.dma_start(emb[:, :], pos_emb).then_inc(s_const, 16)

            def load(i, s, n):
                if not early(i, 2):
                    sp.wait_ge(s_scored, 2 * i - 2)
                head = i // 4
                sp.dma_start(qs[s][:, :, :], q_heads[bass.ds(head, 1), :, bass.ds((i % 4) * 2 * QT, 2 * QT)]
                             .rearrange("a d (x q) -> (a d) x q", x=2)).then_inc(s_qk[s], 16)
                sp.dma_start(ks[s][:, :], k_heads[bass.ds(head, 1)].rearrange("a d t -> (a d) t")).then_inc(s_qk[s], 16)
                if not early(i, 2):
                    sp.wait_ge(s_pv, 2 * i - 1)
                sp.dma_start(vs[s][:, :, :], v_heads[bass.ds(head, 1)].rearrange("a p c d -> (a p) c d")).then_inc(s_v[s], 16)

            load(0, 0, 0)
            with sp.Fori(0, (n_pairs - 2) // 2) as j:
                load(2 * j + 1, 1, j)
                load(2 * j + 2, 0, j + 1)
            load(last, 1, 0)

        @block.tensor
        def _(pe):
            pe.wait_ge(s_const, 32)

            def scores(i, s, x):
                g = 2 * i + x
                if x == 0:
                    pe.wait_ge(s_qk[s], 32 * (i // 2 + 1))
                if not early(g):
                    pe.wait_ge(s_taken, g)
                for n in range(2):
                    mm = nc.tensor.matmul(score_ps[:, n, :], qs[s][:, x, :], ks[s][:, n * 512:(n + 1) * 512],
                                          start=True, stop=True)
                mm = nc.tensor.matmul(table_ps[:, 0:NPOS], qs[s][:, x, :], emb[:, :], start=True, stop=True)
                mm.then_inc(s_scored, 1)

            def turn(i, s, x):
                g = 2 * i + x
                pe.wait_ge(s_exp[x], i + 2)
                pe.wait_ge(s_ptcopy, g + 1)
                for c in range(8):
                    mm = nc.tensor.transpose(pt_ps[:, c, :], logit[s][x][:, c * 128:(c + 1) * 128], ident[:, :])
                mm.then_inc(s_turned, 1)

            def values(i, s, x):
                g = 2 * i + x
                pe.wait_ge(s_ptcopy, g + 2)
                if x == 0:
                    pe.wait_ge(s_v[s], 16 * (i // 2 + 1))
                if x == 0 and not early(i):
                    pe.wait_ge(s_norm[0], i + 1)
                    pe.wait_ge(s_norm[1], i + 1)
                for c in range(8):
                    mm = nc.tensor.matmul(o_ps[:, x * D_HEAD:(x + 1) * D_HEAD], pt[:, c, :], vs[s][:, c, :],
                                          start=(c == 0), stop=(c == 7))
                mm.then_inc(s_pv, 1)

            def step(i, s):
                first, final = early(i), isinstance(i, int) and i == last
                for x in range(2):
                    if not final:
                        scores(i + 1, 1 - s, x)
                    if not first:
                        turn(i - 1, 1 - s, x)
                        values(i - 1, 1 - s, x)

            scores(0, 0, 0)
            scores(0, 0, 1)
            pairs(pe, step)
            for x in range(2):
                turn(last, 1, x)
                values(last, 1, x)

        @block.scalar
        def _(act):
            def take(i, s, x):
                g = 2 * i + x
                act.wait_ge(s_scored, g + 1)
                if not early(i):
                    act.wait_ge(s_scan, g - 1)
                nc.scalar.activation(gate2[x][:, :], score_ps[:, :, :].rearrange("p a b -> p (a b)"), ACT.Tanh, scale=0.5 * SCALE)\
                    .then_inc(s_tabled, 1)
                if not early(i, 2):
                    act.wait_ge(s_pv, g - 2)
                nc.scalar.activation(logit[s][x][:, :], score_ps[:, :, :].rearrange("p a b -> p (a b)"), ACT.Copy, scale=SCALE)
                if not early(i):
                    act.wait_ge(s_pick, 2 * NL * (i - 1) + x + 1)
                nc.scalar.activation(table[x][:, 0:NPOS], table_ps[:, 0:NPOS], ACT.Copy).then_inc(s_taken, 1)

            def spread(i, l, x):
                at = 2 * NL * i + 2 * l + x
                if l == 0:
                    act.wait_ge(s_taken, 2 * i + x + 1)
                if not (early(i) and l == 0):
                    act.wait_ge(s_pick, at - 1)
                if l == NL - 1 and not early(i):
                    act.wait_ge(s_cope, 2 * (i - 1) + x + 1)
                b = LEVELS[l]
                out = window(l, x)
                if l == 0:
                    if early(i) and x == 0:
                        act.wait_ge(s_pad, 1)
                    src = table[x][:, 0:2 * b].unsqueeze(1).to_broadcast([128, SEQ // b, 2 * b])
                    nc.scalar.activation(out, src, ACT.Copy).then_inc(s_copy, 1)
                else:
                    src = window(l - 1, x)[:, :, 0:2 * b].unsqueeze(2).to_broadcast([128, SEQ // b // 2, 2, 2 * b])
                    nc.scalar.activation(out.rearrange("p (j s) e -> p j s e", s=2), src, ACT.Copy).then_inc(s_copy, 1)

            def expo(i, s, x):
                g = 2 * i + x
                act.wait_ge(s_neg, g + 1)
                act.wait_ge(s_rden[x], i + 1)
                nc.scalar.activation(logit[s][x][:, :], logit[s][x][:, :], ACT.Exp, bias=negmax[x][:, :],
                                     accum_out=den[x][:, :]).then_inc(s_exp[x], 1)

            def keep(i, x):
                g = 2 * i + x
                act.wait_ge(s_turned, g + 1)
                act.wait_ge(s_pv, g + 1)
                nc.scalar.activation(pt[:, :, :], pt_ps[:, :, :], ACT.Copy).then_inc(s_ptcopy, 1)

            def norm(i, x):
                g = 2 * i + x
                act.wait_ge(s_pv, 2 * i + 3)
                act.wait_ge(s_rden[x], i + 2)
                act.wait_ge(s_out[x], 16 * (i + 1))
                nc.scalar.activation(o_sb[x][:, :], o_ps[:, x * D_HEAD:(x + 1) * D_HEAD], ACT.Copy, scale=rden[x][:, :])\
                    .then_inc(s_norm[x], 1)
                act.wait_ge(s_norm[x], i + 2)
                act.dma_start(reach(i, x), o_sb[x][:, :]).then_inc(s_out[x], 16)

            def step(i, s):
                first, final = early(i), isinstance(i, int) and i == last
                for l in range(NL):
                    for x in range(2):
                        spread(i, l, x)
                    if l == 2 and not first:
                        for x in range(2):
                            expo(i - 1, 1 - s, x)
                    if l in (3, 4):
                        x = l - 3
                        if not first:
                            keep(i - 1, x)
                        if not final:
                            take(i + 1, 1 - s, x)
                if not first:
                    for x in range(2):
                        norm(i - 1, x)

            take(0, 0, 0)
            take(0, 0, 1)
            pairs(act, step)
            for x in range(2):
                expo(last, 1, x)
            for x in range(2):
                keep(last, x)
            for x in range(2):
                norm(last, x)
            for x in range(2):
                act.wait_ge(s_out[x], 16 * (n_pairs + 1))

        @block.vector
        def _(dve):
            nc.vector.memset(ones[:, :], 1.0).then_inc(s_pad, 1)
            for x in range(2):
                nc.vector.memset(table[x][:, NPOS:PAD], 0.0).then_inc(s_pad, 1)
            dve.wait_ge(s_pad, 3)
            def positions(i, x):
                g = 2 * i + x
                dve.wait_ge(s_tabled, g + 1)
                if not early(i):
                    dve.wait_ge(s_w, g - 1)
                nc.vector.tensor_tensor_scan(pos[x][:, :], gate2[x][:, :], ones[:, 0:1].to_broadcast([128, SEQ]), 0.0,
                                             ALU.add, ALU.add).then_inc(s_scan, 1)
                dve.wait_ge(s_scan, g + 1)
                nc.vector.tensor_scalar(pos[x][:, :], pos[x][:, :], 0.5, float(NPOS - 1), ALU.mult, ALU.min)\
                    .then_inc(s_pos[x], 1)

            def search(i, l, x):
                b = LEVELS[l]
                n = SEQ // b
                here, out = base[x][l], window(l, x)
                at = 5 * i + l
                if not (early(i) and l == 0 and x == 0):
                    dve.wait_ge(s_pick, 2 * NL * i + 2 * l + x)
                if l == 0:
                    dve.wait_ge(s_pos[x], i + 1)
                    r1 = mask_ps[:, 0:n]
                    nc.vector.tensor_scalar(r1, pos[x][:, 0:SEQ:b], float(b), None, ALU.is_ge).then_inc(s_mask[x], 1)
                    dve.wait_ge(s_mask[x], NL * i + 1)
                    nc.vector.tensor_scalar(here[:, :], r1, float(b), None, ALU.mult).then_inc(s_base[x], 1)
                    dve.wait_ge(s_copy, 2 * NL * i + x + 1)
                    mask = bits(r1).unsqueeze(2).to_broadcast([128, n, 2 * b])
                    data = table[x][:, b:3 * b].unsqueeze(1).to_broadcast([128, n, 2 * b])
                    dve.sem_inc(s_held, 1)
                    nc.vector.copy_predicated(out, mask, data).then_inc(s_pick, 1)
                    return
                up, upw = base[x][l - 1], window(l - 1, x)
                upb = up[:, :].unsqueeze(2).to_broadcast([128, n // 2, 2])
                r1 = mask_ps[:, 0:n].rearrange("p (j s) -> p j s", s=2)
                r2 = mask_ps[:, 0:n // 2]
                p2 = pos[x][:, :].rearrange("p (j s b) -> p j s b", s=2, b=b)
                h2 = here[:, :].rearrange("p (j s) -> p j s", s=2)
                o4 = out.rearrange("p (j s) e -> p j s e", s=2)
                dve.wait_ge(s_base[x], at)
                nc.vector.scalar_tensor_tensor(out=r1, in0=p2[:, :, :, 0], scalar=float(b), in1=upb,
                                               op0=ALU.subtract, op1=ALU.is_ge).then_inc(s_mask[x], 1)
                if l == NL - 1 and not early(i):
                    dve.wait_ge(s_cope, 2 * (i - 1) + x + 1)
                dve.wait_ge(s_mask[x], NL * i + l + 1)
                nc.vector.scalar_tensor_tensor(out=h2, in0=r1, scalar=float(b), in1=upb, op0=ALU.mult, op1=ALU.add)\
                    .then_inc(s_base1[x], 1)
                dve.wait_ge(s_copy, 2 * NL * i + 2 * l + x + 1)
                dve.sem_inc(s_held, 1)
                nc.vector.copy_predicated(
                    o4, bits(mask_ps[:, 0:n]).rearrange("p (j s) -> p j s", s=2).unsqueeze(3).to_broadcast([128, n // 2, 2, 2 * b]),
                    upw[:, :, b:3 * b].unsqueeze(2).to_broadcast([128, n // 2, 2, 2 * b])).then_inc(s_pick1[x], 1)
                dve.wait_ge(s_base1[x], at)
                dve.wait_ge(s_pick1[x], at)
                nc.vector.scalar_tensor_tensor(out=r2, in0=p2[:, :, 1, 0], scalar=float(2 * b), in1=up[:, :],
                                               op0=ALU.subtract, op1=ALU.is_ge).then_inc(s_mask2[x], 1)
                dve.wait_ge(s_mask2[x], at)
                nc.vector.scalar_tensor_tensor(out=h2[:, :, 1], in0=r2, scalar=float(b), in1=h2[:, :, 1],
                                               op0=ALU.mult, op1=ALU.add).then_inc(s_leaf if l == NL - 1 else s_base[x], 1)
                nc.vector.copy_predicated(o4[:, :, 1, :], bits(r2).unsqueeze(2).to_broadcast([128, n // 2, 2 * b]),
                                          upw[:, :, 2 * b:4 * b]).then_inc(s_pick, 1)

            def total(i, s, x):
                g = 2 * i + x
                dve.wait_ge(s_cope, g + 1)
                dve.wait_ge(s_taken, g + 1)
                dve.wait_ge(s_exp[x], i + 1)
                dve.sem_inc(s_held, 1)
                nc.vector.tensor_tensor_reduce(logit[s][x][:, :], interp[x][:, :], logit[s][x][:, :], 1.0, -3.0e38,
                                               ALU.add, ALU.max, rowmax[x][:, :]).then_inc(s_z, 1)
                dve.wait_ge(s_z, g + 1)
                nc.vector.tensor_scalar(negmax[x][:, :], rowmax[x][:, :], -1.0, None, ALU.mult).then_inc(s_neg, 1)

            def recip(i, x):
                g = 2 * i + x
                dve.wait_ge(s_exp[x], i + 2)
                dve.wait_ge(s_norm[x], i + 1)
                nc.vector.reciprocal(rden[x][:, :], den[x][:, :]).then_inc(s_rden[x], 1)

            def step(i, s):
                first = early(i)
                for x in range(2):
                    positions(i, x)
                for l in range(NL):
                    for x in range(2):
                        search(i, l, x)
                    if l == 1 and not first:
                        for x in range(2):
                            total(i - 1, 1 - s, x)
                    if l == 4 and not first:
                        for x in range(2):
                            recip(i - 1, x)

            pairs(dve, step)
            for x in range(2):
                total(last, 1, x)
            for x in range(2):
                recip(last, x)

        @block.gpsimd
        def _(pool):
            def leaf(i, s, x):
                g = 2 * i + x
                u = base[x][NL - 1]
                w2 = win[x][2][:, :].rearrange("p (t e) -> p t e", e=2)
                pool.wait_ge(s_leaf, g + 1)
                nc.gpsimd.tensor_tensor(u[:, :], pos[x][:, :], u[:, :], ALU.subtract).then_inc(s_w, 1)
                pool.wait_ge(s_pick, 2 * NL * i + 2 * (NL - 1) + x + 1)
                if not early(i):
                    pool.wait_ge(s_z, g - 1)
                nc.gpsimd.tensor_tensor(interp[x][:, :], w2[:, :, 1], w2[:, :, 0], ALU.subtract).then_inc(s_pool, 1)
                pool.wait_ge(s_w, g + 1)
                pool.wait_ge(s_pool, 2 * g + 1)
                nc.gpsimd.tensor_tensor(interp[x][:, :], interp[x][:, :], u[:, :], ALU.mult).then_inc(s_pool, 1)
                pool.wait_ge(s_pool, 2 * g + 2)
                nc.gpsimd.tensor_tensor(interp[x][:, :], interp[x][:, :], w2[:, :, 0], ALU.add).then_inc(s_cope, 1)

            def step(i, s):
                leaf(i, s, 0)
                leaf(i, s, 1)

            pairs(pool, step)


def build_cross_output(nc, att_rows, x1_rows, wo_t, bo, ln_g, ln_b, x2_rows, z_t, z_sums, ident_dram):
    with ExitStack() as ctx:
        sb, ps, sem, sems = allocators(nc, ctx)
        w_o = sb("r_wo", [128, KT, D])
        bo_row, ones, ident = sb("r_bo", [1, D]), sb("r_ones", [1, 128]), sb("r_ident", [128, 128])
        gain, shift = sb("r_gain", [128, D]), sb("r_shift", [128, D])
        att, aT, x1, x2, y, z, zT = ([sb(f"r_{n}{x}", [128, D]) for x in range(2)] for n in (
            "att", "aT", "x1", "x2", "y", "z", "zT"))
        zsum = sb("r_zsum", [128, D])
        turn_ps, f_ps, turn2_ps = ([ps(f"r_{n}{x}", [128, KT, 128]) for x in range(2)] for n in ("tps", "fps", "t2ps"))
        s_w, s_ones = sem("r_w"), sem("r_ones")
        s_turn, s_aT, s_f, s_x2, s_y, s_zn, s_zg, s_z, s_added, s_turn2, s_zT = (
            slots(sem, f"r_s{n}") for n in ("turn", "aT", "f", "x2", "y", "zn", "zg", "z", "added", "turn2", "zT"))
        s_att, s_x1, s_x2out, s_zout = (dma_slots(sem, f"r_s{n}") for n in ("att", "x1", "x2out", "zout"))
        s_zero, s_sumout = sem("r_zero"), sem("r_sumout", 16)
        n1, n2 = norm_buffers(sb, sem, "r_n1"), norm_buffers(sb, sem, "r_n2")
        block = open_block(nc, ctx, sems)
        PER = ROW_TILES // B // 2

        @block.sync
        def _(sp):
            sp.dma_start(ident[:, :], ident_dram).then_inc(s_w, 16)
            sp.dma_start(w_o[:, :, :], wo_t.rearrange("(k p) n -> p k n", p=128)).then_inc(s_w, 16)
            sp.dma_start(bo_row[:, :], bo.rearrange("(a n) -> a n", a=1)).then_inc(s_w, 16)
            for dst, a in ((gain, ln_g), (shift, ln_b)):
                sp.dma_start(dst[:, :], a.rearrange("(a n) -> a n", a=1).to_broadcast([128, D])).then_inc(s_w, 16)
            with sp.Fori(0, B) as b:
                with sp.Fori(0, PER) as jj:
                    j = b * PER + jj
                    for x in range(2):
                        sp.wait_ge(s_turn[x], j + 1)
                        sp.dma_start(att[x][:, :], row_tile(att_rows, j, x)).then_inc(s_att[x], 16)
                        sp.wait_ge(s_x2[x], j + 1)
                        sp.dma_start(x1[x][:, :], row_tile(x1_rows, j, x)).then_inc(s_x1[x], 16)
                    for x in range(2):
                        sp.wait_ge(s_x2[x], j + 2)
                        sp.dma_start(row_tile(x2_rows, j, x), x2[x][:, :]).then_inc(s_x2out[x], 16)
                    for x in range(2):
                        sp.wait_ge(s_zT[x], j + 2)
                        dst = z_t[bass.ds(b, 1), :, bass.ds((2 * jj + x) * 128, 128)]
                        sp.dma_start(dst.rearrange("a (k p) t -> (a p) k t", p=128),
                                     zT[x][:, :].rearrange("p (k t) -> p k t", k=KT)).then_inc(s_zout[x], 16)
                sp.wait_ge(s_added[1], (b + 1) * PER + 1)
                sp.dma_start(z_sums[bass.ds(b, 1)].rearrange("a p n -> (a p) n"), zsum[:, :]).then_inc(s_sumout, 16)
            for s in (s_x2out, s_zout):
                for x in range(2):
                    sp.wait_ge(s[x], 16 * (ROW_TILES // 2 + 1))
            sp.wait_ge(s_sumout, 16 * (B + 1))

        @block.vector
        def _(dve):
            nc.vector.memset(ones[:, :], 1.0).then_inc(s_ones, 1)
            dve.wait_ge(s_w, 16 * 5)
            with dve.Fori(0, B) as b:
                dve.wait_ge(s_sumout, 16 * (b + 1))
                nc.vector.memset(zsum[:, :], 0.0).then_inc(s_zero, 1)
                with dve.Fori(0, PER) as jj:
                    j = b * PER + jj
                    for x in range(2):
                        dve.wait_ge(s_f[x], j + 2)
                        dve.wait_ge(s_x1[x], 16 * (j + 2))
                        dve.wait_ge(s_x2out[x], 16 * (j + 1))
                        nc.vector.tensor_tensor(x2[x][:, :], f_ps[x][:, :, :].rearrange("p k n -> p (k n)"), x1[x][:, :], ALU.add)\
                            .then_inc(s_x2[x], 1)
                        dve.wait_ge(s_x2[x], j + 2)
                        norm_measure(nc, dve, n1, x, j, x2[x][:, :])
                    for x in range(2):
                        norm_scale(nc, dve, n1, x, j, y[x][:, :], x2[x][:, :]).then_inc(s_y[x], 1)
                        dve.wait_ge(s_y[x], j + 2)
                        norm_measure(nc, dve, n2, x, j, y[x][:, :])
                    for x in range(2):
                        norm_scale(nc, dve, n2, x, j, y[x][:, :], y[x][:, :]).then_inc(s_zn[x], 1)
                        dve.wait_ge(s_zn[x], j + 2)
                        nc.vector.tensor_tensor(y[x][:, :], y[x][:, :], gain[:, :], ALU.mult).then_inc(s_zg[x], 1)
                        dve.wait_ge(s_zg[x], j + 2)
                        dve.wait_ge(s_turn2[x], j + 1)
                        nc.vector.tensor_tensor(z[x][:, :], y[x][:, :], shift[:, :], ALU.add).then_inc(s_z[x], 1)
                        dve.wait_ge(s_z[x], j + 2)
                        if x:
                            dve.wait_ge(s_added[0], j + 2)
                        else:
                            dve.wait_ge(s_added[1], j + 1)
                            dve.wait_ge(s_zero, b + 1)
                        nc.vector.tensor_tensor(zsum[:, :], zsum[:, :], z[x][:, :], ALU.add).then_inc(s_added[x], 1)

        @block.scalar
        def _(act):
            with act.Fori(0, ROW_TILES // 2) as j:
                for x in range(2):
                    act.wait_ge(s_turn[x], j + 2)
                    act.wait_ge(s_f[x], j + 1)
                    nc.scalar.copy(aT[x][:, :], turn_ps[x][:, :, :].rearrange("p k r -> p (k r)")).then_inc(s_aT[x], 1)
                for n in (n1, n2):
                    for x in range(2):
                        norm_root(nc, act, n, x, j)
                for x in range(2):
                    act.wait_ge(s_turn2[x], j + 2)
                    act.wait_ge(s_zout[x], 16 * (j + 1))
                    nc.scalar.copy(zT[x][:, :], turn2_ps[x][:, :, :].rearrange("p k r -> p (k r)")).then_inc(s_zT[x], 1)

        @block.tensor
        def _(pe):
            pe.wait_ge(s_w, 16 * 5)
            pe.wait_ge(s_ones, 1)
            with pe.Fori(0, ROW_TILES // 2) as j:
                for x in range(2):
                    pe.wait_ge(s_att[x], 16 * (j + 2))
                    pe.wait_ge(s_aT[x], j + 1)
                    for k in range(KT):
                        mm = nc.tensor.transpose(turn_ps[x][:, k, :], att[x][:, k * 128:(k + 1) * 128], ident[:, :])
                    mm.then_inc(s_turn[x], 1)
                for x in range(2):
                    pe.wait_ge(s_aT[x], j + 2)
                    pe.wait_ge(s_x2[x], j + 1)
                    dst = f_ps[x][:, :, :].rearrange("p k n -> p (k n)")
                    for k in range(KT):
                        nc.tensor.matmul(dst, aT[x][:, k * 128:(k + 1) * 128], w_o[:, k, :], start=(k == 0), stop=False)
                    nc.tensor.matmul(dst, ones[:, :], bo_row[:, :], start=False, stop=True).then_inc(s_f[x], 1)
                for x in range(2):
                    pe.wait_ge(s_z[x], j + 2)
                    pe.wait_ge(s_zT[x], j + 1)
                    for k in range(KT):
                        mm = nc.tensor.transpose(turn2_ps[x][:, k, :], z[x][:, k * 128:(k + 1) * 128], ident[:, :])
                    mm.then_inc(s_turn2[x], 1)

        @block.gpsimd
        def _(pool):
            pass


def build_experts(nc, z_sums, bn_g, bn_b, bn_mean, bn_var, wr, br, w_down, b_down, w_up, b_up, z_t, x2_rows, out_rows, ident_dram):
    with ExitStack() as ctx:
        sb, ps, sem, sems = allocators(nc, ctx)
        ident = sb("e_ident", [128, 128])
        zs = sb("e_zs", [128, B, D])
        ones = sb("e_ones", [128, 128])
        cols = sb("e_cols", [128, 4, KT])
        wr_sb, br_row = sb("e_wr", [128, KT, E]), sb("e_br", [1, E])
        wd = sb("e_wd", [128, KT, E, H])
        wu, bd, bu = sb("e_wu", [H, E, D]), sb("e_bd", [H, E]), sb("e_bu", [E, D])
        rstd, mean_col, norm_col = sb("e_rstd", [128, KT]), sb("e_mean", [128, KT, B]), sb("e_norm", [128, KT, B])
        logits, mx, negmx, ex, total, pick = (sb(f"e_{n}", [B, m]) for n, m in (
            ("logits", E), ("mx", 1), ("negmx", 1), ("ex", E), ("total", 1), ("pick", 2 * E + 1)))
        order, first = sb("e_order", [B, E]), sb("e_first", [B, 1])
        placed = sb("e_placed", [B, B, E + 1])
        chosen = sb("e_chosen", [128, B, E + 1])
        row_pick = sb("e_rowpick", [E, B, 128])
        wd_b = [sb(f"e_wdb{b}", [128, KT, H]) for b in range(B)]
        wu_b = [sb(f"e_wub{b}", [H, D]) for b in range(B)]
        bd_b, tmp = sb("e_bdb", [H, B]), sb("e_tmp", [H, E])
        zt = [sb(f"e_zt{n}", [128, KT, 512]) for n in range(2)]
        h_sb = [sb(f"e_h{n}", [H, 512]) for n in range(2)]
        xr = [sb(f"e_xr{n}", [128, 4, D]) for n in range(2)]
        mean_ps, misc_ps = ps("e_meanps", [128, 512]), ps("e_miscps", [128, 512])
        h_ps = [ps(f"e_hps{n}", [128, 512]) for n in range(2)]
        y_ps = [ps(f"e_yps{n}", [128, 512]) for n in range(4)]
        s_in, s_ones, s_mean, s_dve, s_pe, s_act, s_order = (sem(f"e_s{n}") for n in ("in", "ones", "mean", "dve", "pe", "act", "order"))
        s_zt, s_xr, s_h, s_hsb, s_out = (slots(sem, f"e_s{n}", 0) for n in ("zt", "xr", "h", "hsb", "out"))
        s_y = [sem(f"e_sy{n}") for n in range(4)]
        s_ysb = [sem(f"e_sysb{n}") for n in range(4)]
        block = open_block(nc, ctx, sems)
        HALVES = SEQ // 512

        @block.sync
        def _(sp):
            one = lambda a: a.rearrange("(a n) -> a n", a=1)
            with nc.allow_non_contiguous_dma(reason="vectors of 512 as columns"):
                loads = [(ident[:, :], ident_dram), (zs[:, :, :], z_sums.rearrange("b p n -> p b n")),
                         (wr_sb[:, :, :], wr.rearrange("(k p) e -> p k e", p=128)), (br_row[:, :], one(br)),
                         (wu[:, :, :], w_up.rearrange("e h n -> h e n")), (bu[:, :], b_up),
                         (bd[:, :], b_down.rearrange("e h -> h e"))]
                loads += [(cols[:, n, :], a.rearrange("(k p) -> p k", p=128)) for n, a in enumerate((bn_g, bn_b, bn_mean, bn_var))]
                loads += [(wd[:, k, :, :], w_down[:, k * 128:(k + 1) * 128, :].rearrange("e p h -> p e h")) for k in range(KT)]
                for dst, src in loads:
                    sp.dma_start(dst, src).then_inc(s_in, 16)
                assert len(loads) == N_LOADS
            for b in range(B):
                for n in range(HALVES):
                    sp.wait_ge(s_h[n], b)
                    sp.dma_start(zt[n][:, :, :], z_t[b, :, n * 512:(n + 1) * 512].rearrange("(k p) t -> p k t", p=128))\
                        .then_inc(s_zt[n], 16)
                    sp.wait_ge(s_out[n], 16 * b)
                    at = b * SEQ + n * 512
                    sp.dma_start(xr[n][:, :, :], x2_rows[at:at + 512, :].rearrange("(c p) n -> p c n", p=128))\
                        .then_inc(s_xr[n], 16)
                for n in range(HALVES):
                    at = b * SEQ + n * 512
                    for c in range(4):
                        sp.wait_ge(s_ysb[c], 2 * b + n + 1)
                    sp.dma_start(out_rows[at:at + 512, :].rearrange("(c p) n -> p c n", p=128), xr[n][:, :, :])\
                        .then_inc(s_out[n], 16)
            for n in range(HALVES):
                sp.wait_ge(s_out[n], 16 * B)

        @block.gpsimd
        def _(pool):
            nc.gpsimd.iota(order[:, :], pattern=[[-1, E]], base=E, channel_multiplier=0,
                           allow_small_or_imprecise_dtypes=True).then_inc(s_order, 1)

        steps = {}

        @block.vector
        def _(dve):
            done = [0]

            def finished(name=None):
                done[0] += 1
                if name:
                    steps[name] = done[0]
                dve.wait_ge(s_dve, done[0])

            nc.vector.memset(ones[:, :], 1.0).then_inc(s_ones, 1)
            dve.wait_ge(s_in, 16 * N_LOADS)
            nc.vector.tensor_scalar(rstd[:, :], cols[:, 3, :], EPS, None, ALU.add).then_inc(s_dve, 1)
            finished("var")
            dve.wait_ge(s_act, 1)
            nc.vector.reciprocal(rstd[:, :], rstd[:, :]).then_inc(s_dve, 1)
            finished()
            nc.vector.tensor_tensor(rstd[:, :], rstd[:, :], cols[:, 0, :], ALU.mult).then_inc(s_dve, 1)
            finished()
            dve.wait_ge(s_pe, 1)
            nc.vector.tensor_scalar(mean_col[:, :, :], mean_ps[:, 0:KT * B].rearrange("p (k b) -> p k b", b=B),
                                        1.0 / SEQ, None, ALU.mult).then_inc(s_dve, 1)
            finished()
            for k in range(KT):
                nc.vector.tensor_scalar(norm_col[:, k, :], mean_col[:, k, :], cols[:, 2, k:k + 1], rstd[:, k:k + 1],
                                            ALU.subtract, ALU.mult).then_inc(s_dve, 1)
                finished()
                nc.vector.tensor_scalar(norm_col[:, k, :], norm_col[:, k, :], cols[:, 1, k:k + 1], None, ALU.add).then_inc(s_dve, 1)
                finished("norm")
            dve.wait_ge(s_pe, 2)
            nc.vector.tensor_copy(logits[:, :], misc_ps[0:B, 0:E]).then_inc(s_dve, 1)
            finished()
            nc.vector.tensor_reduce(mx[:, :], logits[:, :], AX.X, ALU.max).then_inc(s_dve, 1)
            finished()
            nc.vector.tensor_scalar(negmx[:, :], mx[:, :], -1.0, None, ALU.mult).then_inc(s_dve, 1)
            finished("negmx")
            dve.wait_ge(s_order, 1)
            nc.vector.tensor_scalar(pick[:, 0:E], logits[:, :], mx[:, 0:1], None, ALU.is_equal).then_inc(s_dve, 1)
            finished()
            nc.vector.tensor_tensor(pick[:, 0:E], pick[:, 0:E], order[:, :], ALU.mult).then_inc(s_dve, 1)
            finished()
            nc.vector.tensor_reduce(first[:, :], pick[:, 0:E], AX.X, ALU.max).then_inc(s_dve, 1)
            finished()
            nc.vector.tensor_scalar(pick[:, E:2 * E], order[:, :], first[:, 0:1], None, ALU.is_equal).then_inc(s_dve, 1)
            finished()
            dve.wait_ge(s_act, 2)
            nc.vector.reciprocal(pick[:, 2 * E:2 * E + 1], total[:, :]).then_inc(s_dve, 1)
            finished()
            for b in range(B):
                nc.vector.tensor_scalar(placed[:, b, :], pick[:, E:2 * E + 1], ident[0:B, b:b + 1], None, ALU.mult).then_inc(s_dve, 1)
                finished("placed")
            dve.wait_ge(s_pe, 3)
            nc.vector.tensor_copy(chosen[:, :, :], misc_ps[:, 64:64 + B * (E + 1)].rearrange("p (b e) -> p b e", b=B)).then_inc(s_dve, 1)
            finished()
            nc.vector.tensor_copy(row_pick[:, :, :], mean_ps[0:E, 0:512].rearrange("e (b t) -> e b t", b=B)).then_inc(s_dve, 1)
            finished("rowpick")
            for b in range(B):
                for e in range(E):
                    if e == 0:
                        nc.vector.tensor_scalar(wd_b[b][:, :, :], wd[:, :, e, :], chosen[:, b, e:e + 1], None, ALU.mult).then_inc(s_dve, 1)
                        finished()
                        nc.vector.tensor_scalar(wu_b[b][:, :], wu[:, e, :], chosen[0:H, b, e:e + 1], None, ALU.mult).then_inc(s_dve, 1)
                        finished()
                    else:
                        nc.vector.scalar_tensor_tensor(out=wd_b[b][:, :, :], in0=wd[:, :, e, :], scalar=chosen[:, b, e:e + 1],
                                                           in1=wd_b[b][:, :, :], op0=ALU.mult, op1=ALU.add).then_inc(s_dve, 1)
                        finished()
                        nc.vector.scalar_tensor_tensor(out=wu_b[b][:, :], in0=wu[:, e, :], scalar=chosen[0:H, b, e:e + 1],
                                                           in1=wu_b[b][:, :], op0=ALU.mult, op1=ALU.add).then_inc(s_dve, 1)
                        finished()
                nc.vector.tensor_tensor(tmp[:, :], bd[:, :], chosen[0:H, b, 0:E], ALU.mult).then_inc(s_dve, 1)
                finished()
                nc.vector.tensor_reduce(bd_b[:, b:b + 1], tmp[:, :], AX.X, ALU.add).then_inc(s_dve, 1)
                finished(f"weights{b}")
                for n in range(HALVES):
                    dve.wait_ge(s_xr[n], 16 * (b + 1))
                    for c in range(4):
                        dve.wait_ge(s_y[c], 2 * b + n + 1)
                        nc.vector.scalar_tensor_tensor(out=xr[n][:, c, :], in0=y_ps[c][:, :], scalar=chosen[:, b, E:E + 1],
                                                       in1=xr[n][:, c, :], op0=ALU.mult, op1=ALU.add).then_inc(s_ysb[c], 1)

        @block.scalar
        def _(act):
            act.wait_ge(s_dve, steps["var"])
            nc.scalar.activation(rstd[:, :], rstd[:, :], ACT.Sqrt).then_inc(s_act, 1)
            act.wait_ge(s_dve, steps["negmx"])
            nc.scalar.activation(ex[:, :], logits[:, :], ACT.Exp, bias=negmx[:, :], accum_out=total[:, :]).then_inc(s_act, 1)
            for b in range(B):
                act.wait_ge(s_dve, steps[f"weights{b}"])
                for n in range(HALVES):
                    act.wait_ge(s_h[n], b + 1)
                    if b:
                        act.wait_ge(s_y[3], 2 * (b - 1) + n + 1)
                    nc.scalar.activation(h_sb[n][:, :], h_ps[n][0:H, :], ACT.Relu, bias=bd_b[:, b:b + 1]).then_inc(s_hsb[n], 1)

        @block.tensor
        def _(pe):
            pe.wait_ge(s_in, 16 * N_LOADS)
            pe.wait_ge(s_ones, 1)
            for k in range(KT):
                for b in range(B):
                    mm = nc.tensor.matmul(mean_ps[:, k * B + b:k * B + b + 1], zs[:, b, k * 128:(k + 1) * 128], ones[:, 0:1],
                                          start=True, stop=True)
            mm.then_inc(s_pe, 1)
            pe.wait_ge(s_dve, steps["norm"])
            for k in range(KT):
                nc.tensor.matmul(misc_ps[0:B, 0:E], norm_col[:, k, :], wr_sb[:, k, :], start=(k == 0), stop=False)
            nc.tensor.matmul(misc_ps[0:B, 0:E], ones[0:1, 0:B], br_row[:, :], start=False, stop=True).then_inc(s_pe, 1)
            pe.wait_ge(s_dve, steps["placed"])
            for b in range(B):
                nc.tensor.matmul(mean_ps[0:E, b * 128:(b + 1) * 128], placed[:, b, 0:E], ones[0:B, :], start=True, stop=True)
            nc.tensor.matmul(misc_ps[:, 64:64 + B * (E + 1)], ones[0:B, :], placed[:, :, :].rearrange("p b e -> p (b e)"),
                             start=True, stop=True).then_inc(s_pe, 1)
            pe.wait_ge(s_dve, steps["rowpick"])
            for b in range(B):
                pe.wait_ge(s_dve, steps[f"weights{b}"])
                for n in range(HALVES):
                    pe.wait_ge(s_zt[n], 16 * (b + 1))
                    pe.wait_ge(s_hsb[n], b)
                    for k in range(KT):
                        mm = nc.tensor.matmul(h_ps[n][0:H, :], wd_b[b][:, k, :], zt[n][:, k, :], start=(k == 0), stop=(k == KT - 1))
                    mm.then_inc(s_h[n], 1)
                for n in range(HALVES):
                    pe.wait_ge(s_hsb[n], b + 1)
                    for c in range(4):
                        pe.wait_ge(s_ysb[c], 2 * b + n)
                        nc.tensor.matmul(y_ps[c][:, :], h_sb[n][:, c * 128:(c + 1) * 128], wu_b[b][:, :], start=True, stop=False)
                        nc.tensor.matmul(y_ps[c][:, :], row_pick[:, b, :], bu[:, :], start=False, stop=True).then_inc(s_y[c], 1)


def build_decoder_layer(nc, a):
    def scratch(name, shape):
        return nc.dram_tensor(name, shape, F32).ap()

    xn_rows, ctx_rows, x1_rows, att_rows, x2_rows = (scratch(f"t_{n}", [ROWS, D]) for n in ("xn", "ctx", "x1", "att", "x2"))
    qa, ka = scratch("t_qa", [A_HEADS, DH, SEQ]), scratch("t_ka", [A_HEADS, DH, SEQ])
    va, vb = scratch("t_va", [A_HEADS, 128, 8, DH]), scratch("t_vb", [B * HEADS, 128, 8, DH])
    qb, kb = scratch("t_qb", [B, D, SEQ]), scratch("t_kb", [B, D, SEQ])
    z_t, z_sums = scratch("t_zt", [B, D, SEQ]), scratch("t_zsums", [B, 128, D])
    x_rows, out_rows, ident = a["x"].rearrange("b s d -> (b s) d"), a["out"].rearrange("b s d -> (b s) d"), a["ident"]

    def self_place(i, x, half):
        row = (i // 4) * 64
        col = ((i % 4) * 2 + x) * 2 * DH + half * DH
        return ctx_rows[bass.ds(row, 64), bass.ds(col, DH)]

    def cross_place(i, x):
        head = i // 4
        row = (head // HEADS) * SEQ + ((i % 4) * 2 + x) * QT
        return att_rows[bass.ds(row, QT), bass.ds((head % HEADS) * DH, DH)]

    build_memory_projections(nc, a["ctx_t"], a["xwk"], a["xbk"], a["xwv"], a["xbv"], kb, vb)
    build_self_projections(nc, x_rows, a["wq"], a["bq"], a["wk"], a["bk"], a["wv"], a["bv"], xn_rows, qa, ka, va, ident)
    build_self_attention(nc, qa, ka, va, self_place, ident)
    build_self_output(nc, ctx_rows, xn_rows, x_rows, a["wf"], a["bf"], a["xwq"], a["xbq"], x1_rows, qb, ident)
    build_cope_attention(nc, B * HEADS * 4, qb.rearrange("b (h d) t -> (b h) d t", d=DH),
                         kb.rearrange("b (h d) t -> (b h) d t", d=DH), vb, a["emb"], cross_place, ident)
    build_cross_output(nc, att_rows, x1_rows, a["xwo"], a["xbo"], a["ln_g"], a["ln_b"], x2_rows, z_t, z_sums, ident)
    build_experts(nc, z_sums, a["bn_g"], a["bn_b"], a["bn_mean"], a["bn_var"], a["wr"], a["br"], a["w_down"], a["b_down"],
                  a["w_up"], a["b_up"], z_t, x2_rows, out_rows, ident)


def lay_out(inputs):
    import numpy as np

    n = {k: np.asarray(v) for k, v in inputs.items()}
    attn, xattn, ffn = (lambda k, p=p: n[f"L0_{p}_{k}"] for p in ("attn", "xattn", "ffn"))
    evens = [g * DH + d for par in range(2) for g in range(par, HEADS, 2) for d in range(DH)]
    arrays = {
        "x": n["x"], "ctx_t": n["ctx_1024"][:, ::-1, :].transpose(0, 2, 1),
        "wq": attn("Wq"), "bq": attn("bq"), "wk": attn("Wk"), "bk": attn("bk"),
        "wv": attn("Wv")[:, evens], "bv": attn("bv")[evens], "wf": attn("Wf"), "bf": attn("bf"),
        "xwq": xattn("Wq_w").T, "xbq": xattn("Wq_b"), "xwk": xattn("Wk_w").T, "xbk": xattn("Wk_b"),
        "xwv": xattn("Wv_w").T, "xbv": xattn("Wv_b"), "xwo": xattn("Wo_w").T, "xbo": xattn("Wo_b"),
        "emb": xattn("pos_emb"),
        "ln_g": ffn("ln_g"), "ln_b": ffn("ln_b"), "bn_g": ffn("bn_g"), "bn_b": ffn("bn_b"),
        "bn_mean": ffn("bn_mean"), "bn_var": ffn("bn_var"), "wr": ffn("Wr"), "br": ffn("br"),
        "w_down": ffn("W_down"), "b_down": ffn("b_down"), "w_up": ffn("W_up"), "b_up": ffn("b_up"),
        "ident": np.eye(128, dtype=np.float32),
    }
    return {k: np.ascontiguousarray(v) for k, v in arrays.items()}


def kernel(**inputs):
    import concourse.bacc as bacc
    from concourse.bass_utils import run_bass_kernel_spmd

    nc = bacc.Bacc("TRN2", target_bir_lowering=False, num_devices=1)
    given = lay_out(inputs)
    arrays = {f"in_{k}": v for k, v in given.items()}
    aps = {k: nc.dram_tensor(f"in_{k}", v.shape, mybir.dt.from_np(v.dtype), kind="ExternalInput").ap() for k, v in given.items()}
    aps["out"] = nc.dram_tensor("out_0", (B, SEQ, D), F32, kind="ExternalOutput").ap()
    build_decoder_layer(nc, aps)
    r = run_bass_kernel_spmd(nc, [arrays], core_ids=[0])
    return r.results[0]["out_0"]
```

```python
from contextlib import ExitStack

import concourse.bass as bass
from concourse import mybir

F32 = mybir.dt.float32
U32 = mybir.dt.uint32
ALU = mybir.AluOpType
ACT = mybir.ActivationFunctionType
AX = mybir.AxisListType

B, SEQ, D = 4, 1024, 512
ROWS = B * SEQ
ROW_TILES = ROWS // 128
KT = D // 128
HEADS, DH = 16, 32
A_HEADS = B * HEADS
A_SCALE = 8.0
E, H = 8, 64
N_LOADS = 15
EPS = 1e-5
D_HEAD = DH
NPOS = 64
QT = 128
LEVELS = [32, 16, 8, 4, 2]
NL = len(LEVELS)
PAD = 96
SCALE = 1.0 / float(DH) ** 0.5

def allocators(nc, ctx):
    sems = []

    def sb(name, shape, dt=F32):
        return ctx.enter_context(nc.sbuf_tensor(name, shape, dt))

    def ps(name, shape, dt=F32):
        return ctx.enter_context(nc.psum_tensor(name, shape, dt))

    def sem(name, at_first=0):
        sems.append((ctx.enter_context(nc.semaphore(name)), at_first))
        return sems[-1][0]

    return sb, ps, sem, sems


def open_block(nc, ctx, sems):
    def clear():
        for s, _ in sems:
            nc.gpsimd.sem_clear(s)
        nc.all_engine_barrier()

    for s, at_first in sems:
        if at_first:
            nc.gpsimd.sem_inc(s, at_first)
    nc.all_engine_barrier()
    ctx.callback(clear)
    return ctx.enter_context(nc.Block())


def slots(sem, name, at_first=1):
    return [sem(f"{name}{x}", at_first) for x in range(2)]


def dma_slots(sem, name):
    return slots(sem, name, 16)


def norm_buffers(sb, sem, name):
    t = {n: [sb(f"{name}_{n}{x}", [128, m]) for x in range(2)] for n, m in (("stats", 6), ("mv", 2), ("std", 1), ("rstd", 1))}
    for n in ("s_stats", "s_mv", "s_var", "s_std", "s_rstd"):
        t[n] = slots(sem, f"{name}_{n}")
    t["s_held"] = sem(f"{name}_held")
    return t


def norm_measure(nc, dve, t, x, j, rows):
    nc.vector.bn_stats(t["stats"][x][:, :], rows).then_inc(t["s_stats"][x], 1)
    dve.wait_ge(t["s_stats"][x], j + 2)
    dve.sem_inc(t["s_held"], 1)
    nc.vector.bn_aggr(t["mv"][x][:, :], t["stats"][x][:, :]).then_inc(t["s_mv"][x], 1)
    dve.wait_ge(t["s_mv"][x], j + 2)
    nc.vector.tensor_scalar(t["mv"][x][:, 1:2], t["mv"][x][:, 1:2], EPS, None, ALU.add).then_inc(t["s_var"][x], 1)


def norm_root(nc, act, t, x, j):
    act.wait_ge(t["s_var"][x], j + 2)
    nc.scalar.activation(t["std"][x][:, :], t["mv"][x][:, 1:2], ACT.Sqrt).then_inc(t["s_std"][x], 1)


def norm_scale(nc, dve, t, x, j, out, rows):
    dve.wait_ge(t["s_std"][x], j + 2)
    nc.vector.reciprocal(t["rstd"][x][:, :], t["std"][x][:, :]).then_inc(t["s_rstd"][x], 1)
    dve.wait_ge(t["s_rstd"][x], j + 2)
    return nc.vector.tensor_scalar(out, rows, t["mv"][x][:, 0:1], t["rstd"][x][:, 0:1], ALU.subtract, ALU.mult)


def build_memory_projections(nc, ctx_t, wk_t, bk, wv_t, bv, k_heads, v_heads):
    with ExitStack() as ctx:
        sb, ps, sem, sems = allocators(nc, ctx)
        wk, wv = (sb(f"m_w{n}", [128, KT, D]) for n in "kv")
        bk_row, bv_row = (sb(f"m_b{n}", [1, D]) for n in "kv")
        ones = sb("m_ones", [1, 512])
        tokens = sb("m_tokens", [128, KT, SEQ])
        out_sb = [sb(f"m_out{n}", [128, 512]) for n in range(4)]
        acc = [ps(f"m_acc{n}", [128, 512]) for n in range(4)]
        s_w, s_ones, s_tokens, s_used = sem("m_w"), sem("m_ones"), sem("m_tokens"), sem("m_used", 1)
        s_acc = [sem(f"m_acc{n}") for n in range(4)]
        s_sb = [sem(f"m_sb{n}", 1) for n in range(4)]
        s_out = [sem(f"m_outs{n}", 16) for n in range(4)]
        block = open_block(nc, ctx, sems)
        GROUPS = 16

        @block.sync
        def _(sp):
            for dst, src in ((wk, wk_t), (wv, wv_t)):
                sp.dma_start(dst[:, :, :], src.rearrange("(k p) n -> p k n", p=128)).then_inc(s_w, 16)
            for dst, src in ((bk_row, bk), (bv_row, bv)):
                sp.dma_start(dst[:, :], src.rearrange("(a n) -> a n", a=1)).then_inc(s_w, 16)
            with sp.Fori(0, B) as b:
                sp.wait_ge(s_used, b + 1)
                sp.dma_start(tokens[:, :, :], ctx_t[bass.ds(b, 1)].rearrange("a (k p) t -> (a p) k t", p=128))\
                    .then_inc(s_tokens, 16)
                for g in range(GROUPS):
                    n = g % 4
                    sp.wait_ge(s_sb[n], 4 * b + g // 4 + 2)
                    if g < 8:
                        f, half = g // 2, g % 2
                        dst = k_heads[bass.ds(b, 1), f * 128:(f + 1) * 128, half * 512:(half + 1) * 512]
                        sp.dma_start(dst.rearrange("a p t -> (a p) t"), out_sb[n][:, :]).then_inc(s_out[n], 16)
                    else:
                        dst = v_heads[bass.ds(b * HEADS, HEADS), :, g - 8, :]
                        sp.dma_start(dst.rearrange("h p d -> p h d"),
                                     out_sb[n][:, :].rearrange("p (h d) -> p h d", h=HEADS)).then_inc(s_out[n], 16)
            for n in range(4):
                sp.wait_ge(s_out[n], 16 * (4 * B + 1))

        @block.tensor
        def _(pe):
            pe.wait_ge(s_w, 64)
            pe.wait_ge(s_ones, 1)
            with pe.Fori(0, B) as b:
                pe.wait_ge(s_tokens, 16 * (b + 1))
                for g in range(GROUPS):
                    n = g % 4
                    pe.wait_ge(s_sb[n], 4 * b + g // 4 + 1)
                    for k in range(KT):
                        if g < 8:
                            f, half = g // 2, g % 2
                            nc.tensor.matmul(acc[n][:, :], wk[:, k, f * 128:(f + 1) * 128],
                                             tokens[:, k, half * 512:(half + 1) * 512], start=(k == 0), stop=False)
                        else:
                            c = g - 8
                            nc.tensor.matmul(acc[n][:, :], tokens[:, k, c * 128:(c + 1) * 128], wv[:, k, :],
                                             start=(k == 0), stop=False)
                    if g < 8:
                        mm = nc.tensor.matmul(acc[n][:, :], bk_row[:, f * 128:(f + 1) * 128], ones[:, :],
                                              start=False, stop=True)
                    else:
                        mm = nc.tensor.matmul(acc[n][:, :], ones[:, 0:128], bv_row[:, :], start=False, stop=True)
                    mm.then_inc(s_acc[n], 1)
                pe.wait_ge(s_acc[(GROUPS - 1) % 4], 4 * (b + 1))
                pe.sem_inc(s_used, 1)

        def drain(eng, copy, mine):
            with eng.Fori(0, B) as b:
                for g in mine:
                    n = g % 4
                    eng.wait_ge(s_acc[n], 4 * b + g // 4 + 1)
                    eng.wait_ge(s_out[n], 16 * (4 * b + g // 4 + 1))
                    copy(out_sb[n][:, :], acc[n][:, :]).then_inc(s_sb[n], 1)

        @block.vector
        def _(dve):
            nc.vector.memset(ones[:, :], 1.0).then_inc(s_ones, 1)
            drain(dve, nc.vector.tensor_copy, range(0, GROUPS, 2))

        @block.scalar
        def _(act):
            drain(act, nc.scalar.copy, range(1, GROUPS, 2))

        @block.gpsimd
        def _(pool):
            pass


def row_tile(a, j, x):
    return a[bass.ds((2 * j + x) * 128, 128), :]


def build_self_projections(nc, x_rows, wq, bq, wk, bk, wv, bv, xn_rows, q_heads, k_heads, v_heads, ident_dram):
    with ExitStack() as ctx:
        sb, ps, sem, sems = allocators(nc, ctx)
        w = {n: sb(f"s_w{n}", [128, KT, D]) for n in "qkv"}
        brow = {n: sb(f"s_b{n}", [1, D]) for n in "qkv"}
        ones = sb("s_ones", [1, 128])
        ident = sb("s_ident", [128, 128])
        xt, xn, xT = ([sb(f"s_{n}{x}", [128, D]) for x in range(2)] for n in ("xt", "xn", "xT"))
        qk_sb = {n: [sb(f"s_{n}sb{x}", [DH, 2, HEADS, 64]) for x in range(2)] for n in "qk"}
        v_sb = [sb(f"s_vsb{x}", [128, 2, 256]) for x in range(2)]
        turn_ps = [ps(f"s_turn{x}", [128, KT, 128]) for x in range(2)]
        out_ps = {n: [ps(f"s_{n}ps{x}", [128, 512]) for x in range(2)] for n in "qkv"}
        s_w, s_ones = sem("s_wload"), sem("s_ones")
        s_xn, s_turn, s_xT, s_mm, s_evq, s_evk, s_evv = (
            slots(sem, f"s_s{n}") for n in ("xn", "turn", "xT", "mm", "evq", "evk", "evv"))
        s_x, s_xnout, s_outq, s_outk, s_outv = (dma_slots(sem, f"s_s{n}") for n in ("x", "xnout", "outq", "outk", "outv"))
        norm = norm_buffers(sb, sem, "s_n")
        block = open_block(nc, ctx, sems)

        @block.sync
        def _(sp):
            sp.dma_start(ident[:, :], ident_dram).then_inc(s_w, 16)
            for n, a in (("q", wq), ("k", wk), ("v", wv)):
                sp.dma_start(w[n][:, :, :], a.rearrange("(k p) n -> p k n", p=128)).then_inc(s_w, 16)
            for n, a in (("q", bq), ("k", bk), ("v", bv)):
                sp.dma_start(brow[n][:, :], a.rearrange("(a n) -> a n", a=1)).then_inc(s_w, 16)
            with sp.Fori(0, ROW_TILES // 2) as j:
                for x in range(2):
                    sp.wait_ge(s_xn[x], j + 1)
                    sp.dma_start(xt[x][:, :], row_tile(x_rows, j, x)).then_inc(s_x[x], 16)
                for x in range(2):
                    sp.wait_ge(s_xn[x], j + 2)
                    sp.dma_start(row_tile(xn_rows, j, x), xn[x][:, :]).then_inc(s_xnout[x], 16)
                for x in range(2):
                    head = 4 * j + 2 * x
                    for n, dst, s_ev, s_out in (("q", q_heads, s_evq, s_outq), ("k", k_heads, s_evk, s_outk)):
                        sp.wait_ge(s_ev[x], j + 2)
                        sp.dma_start(dst[bass.ds(head, 2)].rearrange("h d t -> d h t"),
                                     qk_sb[n][x][:, :, :, :].rearrange("d h c r -> d h (c r)")).then_inc(s_out[x], 16)
                    sp.wait_ge(s_evv[x], j + 2)
                    sp.dma_start(v_heads[bass.ds(head, 2)].rearrange("h p c d -> p h (c d)"), v_sb[x][:, :, :])\
                        .then_inc(s_outv[x], 16)
            for s in (s_xnout, s_outq, s_outk, s_outv):
                for x in range(2):
                    sp.wait_ge(s[x], 16 * (ROW_TILES // 2 + 1))

        @block.vector
        def _(dve):
            nc.vector.memset(ones[:, :], 1.0).then_inc(s_ones, 1)
            with dve.Fori(0, ROW_TILES // 2) as j:
                for x in range(2):
                    dve.wait_ge(s_x[x], 16 * (j + 2))
                    norm_measure(nc, dve, norm, x, j, xt[x][:, :])
                for x in range(2):
                    dve.wait_ge(s_xnout[x], 16 * (j + 1))
                    dve.wait_ge(s_turn[x], j + 1)
                    norm_scale(nc, dve, norm, x, j, xn[x][:, :], xt[x][:, :]).then_inc(s_xn[x], 1)
                for x in range(2):
                    dve.wait_ge(s_mm[x], j + 2)
                    dve.wait_ge(s_outk[x], 16 * (j + 1))
                    for c4 in range(4):
                        ins = nc.vector.tensor_copy(
                            qk_sb["k"][x][:, :, :, :].rearrange("d h (o c) r -> d o c h r", c=4)[:, :, c4],
                            out_ps["k"][x][c4 * DH:(c4 + 1) * DH, :].rearrange("p (o h r) -> p o h r", h=2, r=64))
                    ins.then_inc(s_evk[x], 1)
                    dve.wait_ge(s_outv[x], 16 * (j + 1))
                    nc.vector.tensor_copy(v_sb[x][:, :, :], out_ps["v"][x][:, :].rearrange("p (h n) -> p h n", h=2))\
                        .then_inc(s_evv[x], 1)

        @block.scalar
        def _(act):
            with act.Fori(0, ROW_TILES // 2) as j:
                for x in range(2):
                    norm_root(nc, act, norm, x, j)
                for x in range(2):
                    act.wait_ge(s_turn[x], j + 2)
                    act.wait_ge(s_mm[x], j + 1)
                    nc.scalar.copy(xT[x][:, :], turn_ps[x][:, :, :].rearrange("p k r -> p (k r)")).then_inc(s_xT[x], 1)
                for x in range(2):
                    act.wait_ge(s_mm[x], j + 2)
                    act.wait_ge(s_outq[x], 16 * (j + 1))
                    for c4 in range(4):
                        ins = nc.scalar.copy(
                            qk_sb["q"][x][:, :, :, :].rearrange("d h (o c) r -> d o c h r", c=4)[:, :, c4],
                            out_ps["q"][x][c4 * DH:(c4 + 1) * DH, :].rearrange("p (o h r) -> p o h r", h=2, r=64))
                    ins.then_inc(s_evq[x], 1)

        @block.tensor
        def _(pe):
            pe.wait_ge(s_w, 16 * 7)
            pe.wait_ge(s_ones, 1)
            with pe.Fori(0, ROW_TILES // 2) as j:
                for x in range(2):
                    pe.wait_ge(s_xn[x], j + 2)
                    pe.wait_ge(s_xT[x], j + 1)
                    for k in range(KT):
                        mm = nc.tensor.transpose(turn_ps[x][:, k, :], xn[x][:, k * 128:(k + 1) * 128], ident[:, :])
                    mm.then_inc(s_turn[x], 1)
                for x in range(2):
                    pe.wait_ge(s_xT[x], j + 2)
                    pe.wait_ge(s_evq[x], j + 1)
                    pe.wait_ge(s_evk[x], j + 1)
                    for n in "qk":
                        for o in range(4):
                            dst = out_ps[n][x][:, o * 128:(o + 1) * 128]
                            for k in range(KT):
                                nc.tensor.matmul(dst, w[n][:, k, o * 128:(o + 1) * 128], xT[x][:, k * 128:(k + 1) * 128],
                                                 start=(k == 0), stop=False)
                            nc.tensor.matmul(dst, brow[n][:, o * 128:(o + 1) * 128], ones[:, :], start=False, stop=True)
                    pe.wait_ge(s_evv[x], j + 1)
                    for h in range(2):
                        for odd in range(2):
                            dst = out_ps["v"][x][odd * 64:(odd + 1) * 64, h * 256:(h + 1) * 256]
                            for k in range(KT):
                                nc.tensor.matmul(dst, xT[x][:, k * 128 + h * 64:k * 128 + (h + 1) * 64],
                                                 w["v"][:, k, odd * 256:(odd + 1) * 256], start=(k == 0), stop=False)
                            mm = nc.tensor.matmul(dst, ones[:, 0:64], brow["v"][:, odd * 256:(odd + 1) * 256],
                                                  start=False, stop=True)
                    mm.then_inc(s_mm[x], 1)

        @block.gpsimd
        def _(pool):
            pass


def build_self_attention(nc, q_heads, k_heads, v_heads, reach, ident_dram):
    with ExitStack() as ctx:
        sb, ps, sem, sems = allocators(nc, ctx)
        ident = sb("a_ident", [128, 128])
        qs = [sb(f"a_q{s}", [DH, 2, QT]) for s in range(2)]
        ks = [sb(f"a_k{s}", [DH, SEQ]) for s in range(2)]
        vs = [sb(f"a_v{s}", [128, 8, DH]) for s in range(2)]
        probs = [sb(f"a_probs{x}", [128, SEQ]) for x in range(2)]
        pt = [sb(f"a_pt{x}", [128, 8, QT]) for x in range(2)]
        rowmax, bias, den, rden = ([sb(f"a_{n}{x}", [128, 1]) for x in range(2)] for n in ("max", "bias", "den", "rden"))
        o_sb = [sb(f"a_o{x}", [128, DH]) for x in range(2)]
        score_ps = [ps(f"a_score{x}", [128, 2, 512]) for x in range(2)]
        pt_ps = ps("a_ptps", [128, 8, QT])
        o_ps = [ps(f"a_ops{x}", [128, 512]) for x in range(2)]
        s_const = sem("a_const")
        s_qk, s_v = slots(sem, "a_qk", 0), slots(sem, "a_vload", 0)
        (s_scored, s_max, s_bias, s_exp, s_turned, s_kept_a, s_kept_d, s_pv, s_rden, s_norm) = (
            sem(f"a_s{n}") for n in ("scored", "max", "bias", "exp", "turned", "kept_a", "kept_d", "pv", "rden", "norm"))
        s_out = dma_slots(sem, "a_out")
        block = open_block(nc, ctx, sems)
        n_pairs = A_HEADS * 4
        last = n_pairs - 1

        def pairs(eng, step):
            step(0, 0)
            with eng.Fori(0, (n_pairs - 2) // 2) as j:
                step(2 * j + 1, 1)
                step(2 * j + 2, 0)
            step(last, 1)

        def early(i, n=1):
            return isinstance(i, int) and i < n

        @block.sync
        def _(sp):
            sp.dma_start(ident[:, :], ident_dram).then_inc(s_const, 16)

            def load(i, s):
                if not early(i, 2):
                    sp.wait_ge(s_scored, 2 * i - 2)
                head = i // 4
                sp.dma_start(qs[s][:, :, :], q_heads[bass.ds(head, 1), :, bass.ds((i % 4) * 2 * QT, 2 * QT)]
                             .rearrange("a d (x q) -> (a d) x q", x=2)).then_inc(s_qk[s], 16)
                sp.dma_start(ks[s][:, :], k_heads[bass.ds(head, 1)].rearrange("a d t -> (a d) t")).then_inc(s_qk[s], 16)
                if not early(i, 2):
                    sp.wait_ge(s_pv, 2 * i - 2)
                sp.dma_start(vs[s][:, :, :], v_heads[bass.ds(head, 1)].rearrange("a p c d -> (a p) c d")).then_inc(s_v[s], 16)

            pairs(sp, load)

        @block.tensor
        def _(pe):
            pe.wait_ge(s_const, 16)

            def scores(i, s, x):
                g = 2 * i + x
                if x == 0:
                    pe.wait_ge(s_qk[s], 32 * (i // 2 + 1))
                if not early(i):
                    pe.wait_ge(s_exp, g - 1)
                for n in range(2):
                    mm = nc.tensor.matmul(score_ps[x][:, n, :], qs[s][:, x, :], ks[s][:, n * 512:(n + 1) * 512],
                                          start=True, stop=True)
                mm.then_inc(s_scored, 1)

            def turn(i, x):
                g = 2 * i + x
                pe.wait_ge(s_exp, g + 1)
                if not early(g):
                    pe.wait_ge(s_kept_a, g)
                    pe.wait_ge(s_kept_d, g)
                for c in range(8):
                    mm = nc.tensor.transpose(pt_ps[:, c, :], probs[x][:, c * 128:(c + 1) * 128], ident[:, :])
                mm.then_inc(s_turned, 1)

            def values(i, s, x):
                g = 2 * i + x
                pe.wait_ge(s_kept_a, g + 1)
                pe.wait_ge(s_kept_d, g + 1)
                if x == 0:
                    pe.wait_ge(s_v[s], 16 * (i // 2 + 1))
                if x or not early(i):
                    pe.wait_ge(s_norm, g if x else g - 1)
                for c in range(8):
                    mm = nc.tensor.matmul(o_ps[x][:, 0:DH], pt[x][:, c, :], vs[s][:, c, :], start=(c == 0), stop=(c == 7))
                mm.then_inc(s_pv, 1)

            def step(i, s):
                first, final = early(i), isinstance(i, int) and i == last
                scores(i, s, 1)
                if not first:
                    values(i - 1, 1 - s, 1)
                turn(i, 0)
                if not final:
                    scores(i + 1, 1 - s, 0)
                values(i, s, 0)
                turn(i, 1)

            scores(0, 0, 0)
            pairs(pe, step)
            values(last, 1, 1)

        @block.vector
        def _(dve):
            def peak(i, x):
                g = 2 * i + x
                dve.wait_ge(s_scored, g + 1)
                nc.vector.tensor_reduce(rowmax[x][:, :], score_ps[x][:, :, :], AX.XY, ALU.max).then_inc(s_max, 1)
                if not early(i):
                    dve.wait_ge(s_exp, g - 1)
                dve.wait_ge(s_max, g + 1)
                nc.vector.tensor_scalar(bias[x][:, :], rowmax[x][:, :], -A_SCALE, None, ALU.mult).then_inc(s_bias, 1)

            def keep(i, x):
                g = 2 * i + x
                dve.wait_ge(s_turned, g + 1)
                if not early(i):
                    dve.wait_ge(s_pv, g - 1)
                nc.vector.tensor_copy(pt[x][:, 0:4, :], pt_ps[:, 0:4, :]).then_inc(s_kept_d, 1)

            def norm(i, x):
                g = 2 * i + x
                dve.wait_ge(s_exp, g + 1)
                if x or not early(i):
                    dve.wait_ge(s_norm, g if x else g - 1)
                nc.vector.reciprocal(rden[x][:, :], den[x][:, :]).then_inc(s_rden, 1)
                dve.wait_ge(s_pv, g + 1)
                dve.wait_ge(s_rden, g + 1)
                dve.wait_ge(s_out[x], 32 * i + 16)
                nc.vector.tensor_scalar(o_sb[x][:, :], o_ps[x][:, 0:DH], rden[x][:, 0:1], None, ALU.mult).then_inc(s_norm, 1)

            def step(i, s):
                first, final = early(i), isinstance(i, int) and i == last
                peak(i, 1)
                keep(i, 0)
                if not first:
                    norm(i - 1, 1)
                if not final:
                    peak(i + 1, 0)
                keep(i, 1)
                norm(i, 0)

            peak(0, 0)
            pairs(dve, step)
            norm(last, 1)

        @block.scalar
        def _(act):
            def expo(i, x):
                g = 2 * i + x
                act.wait_ge(s_bias, g + 1)
                if not early(i):
                    act.wait_ge(s_turned, g - 1)
                    act.wait_ge(s_rden, g - 1)
                nc.scalar.activation(probs[x][:, :], score_ps[x][:, :, :].rearrange("p a b -> p (a b)"), ACT.Exp,
                                     bias=bias[x][:, :], scale=A_SCALE, accum_out=den[x][:, :]).then_inc(s_exp, 1)

            def keep(i, x):
                g = 2 * i + x
                act.wait_ge(s_turned, g + 1)
                if not early(i):
                    act.wait_ge(s_pv, g - 1)
                nc.scalar.copy(pt[x][:, 4:8, :], pt_ps[:, 4:8, :]).then_inc(s_kept_a, 1)

            def send(i, x):
                g = 2 * i + x
                act.wait_ge(s_norm, g + 1)
                for half in range(2):
                    act.dma_start(reach(i, x, half), o_sb[x][half * 64:(half + 1) * 64, :]).then_inc(s_out[x], 16)

            def step(i, s):
                first, final = early(i), isinstance(i, int) and i == last
                expo(i, 1)
                keep(i, 0)
                if not first:
                    send(i - 1, 1)
                if not final:
                    expo(i + 1, 0)
                keep(i, 1)
                send(i, 0)

            expo(0, 0)
            pairs(act, step)
            send(last, 1)
            for x in range(2):
                act.wait_ge(s_out[x], 32 * n_pairs + 16)

        @block.gpsimd
        def _(pool):
            pass


def build_self_output(nc, ctx_rows, xn_rows, x_rows, wf, bf, wq_t, bq, x1_rows, q_heads, ident_dram):
    with ExitStack() as ctx:
        sb, ps, sem, sems = allocators(nc, ctx)
        w_f, w_q = sb("o_wf", [128, KT, D]), sb("o_wq", [128, KT, D])
        bf_row, bq_row = sb("o_bf", [1, D]), sb("o_bq", [1, D])
        ones, ident = sb("o_ones", [1, 128]), sb("o_ident", [128, 128])
        att, xn, xr, cn, cT, x1, x1n, x1T, q_sb = ([sb(f"o_{n}{x}", [128, D]) for x in range(2)] for n in (
            "att", "xn", "xr", "cn", "cT", "x1", "x1n", "x1T", "qsb"))
        turn_ps, f_ps, turn2_ps, q_ps = ([ps(f"o_{n}{x}", [128, KT, 128]) for x in range(2)] for n in ("tps", "fps", "t2ps", "qps"))
        s_w, s_ones = sem("o_w"), sem("o_ones")
        s_sum, s_cn, s_turn, s_cT, s_f, s_x1, s_x1n, s_turn2, s_x1T, s_q, s_qsb = (
            slots(sem, f"o_s{n}") for n in ("sum", "cn", "turn", "cT", "f", "x1", "x1n", "turn2", "x1T", "q", "qsb"))
        s_att, s_xr, s_x1out, s_qout = (dma_slots(sem, f"o_s{n}") for n in ("att", "xr", "x1out", "qout"))
        n1, n2 = norm_buffers(sb, sem, "o_n1"), norm_buffers(sb, sem, "o_n2")
        block = open_block(nc, ctx, sems)

        @block.sync
        def _(sp):
            sp.dma_start(ident[:, :], ident_dram).then_inc(s_w, 16)
            for dst, a in ((w_f, wf), (w_q, wq_t)):
                sp.dma_start(dst[:, :, :], a.rearrange("(k p) n -> p k n", p=128)).then_inc(s_w, 16)
            for dst, a in ((bf_row, bf), (bq_row, bq)):
                sp.dma_start(dst[:, :], a.rearrange("(a n) -> a n", a=1)).then_inc(s_w, 16)
            with sp.Fori(0, ROW_TILES // 2) as j:
                for x in range(2):
                    sp.wait_ge(s_cn[x], j + 1)
                    sp.dma_start(att[x][:, :], row_tile(ctx_rows, j, x)).then_inc(s_att[x], 16)
                    sp.dma_start(xn[x][:, :], row_tile(xn_rows, j, x)).then_inc(s_att[x], 16)
                    sp.wait_ge(s_x1[x], j + 1)
                    sp.dma_start(xr[x][:, :], row_tile(x_rows, j, x)).then_inc(s_xr[x], 16)
                for x in range(2):
                    sp.wait_ge(s_x1[x], j + 2)
                    sp.dma_start(row_tile(x1_rows, j, x), x1[x][:, :]).then_inc(s_x1out[x], 16)
                for x in range(2):
                    sp.wait_ge(s_qsb[x], j + 2)
                    t = 2 * j + x
                    dst = q_heads[bass.ds(t // 8, 1), :, bass.ds((t % 8) * 128, 128)]
                    sp.dma_start(dst.rearrange("a (o p) t -> (a p) o t", p=128),
                                 q_sb[x][:, :].rearrange("p (o t) -> p o t", o=4)).then_inc(s_qout[x], 16)
            for s in (s_x1out, s_qout):
                for x in range(2):
                    sp.wait_ge(s[x], 16 * (ROW_TILES // 2 + 1))

        @block.vector
        def _(dve):
            nc.vector.memset(ones[:, :], 1.0).then_inc(s_ones, 1)
            with dve.Fori(0, ROW_TILES // 2) as j:
                for x in range(2):
                    dve.wait_ge(s_att[x], 32 * (j + 1) + 16)
                    nc.vector.tensor_tensor(att[x][:, :], att[x][:, :], xn[x][:, :], ALU.add).then_inc(s_sum[x], 1)
                    dve.wait_ge(s_sum[x], j + 2)
                    norm_measure(nc, dve, n1, x, j, att[x][:, :])
                for x in range(2):
                    dve.wait_ge(s_turn[x], j + 1)
                    norm_scale(nc, dve, n1, x, j, cn[x][:, :], att[x][:, :]).then_inc(s_cn[x], 1)
                for x in range(2):
                    dve.wait_ge(s_f[x], j + 2)
                    dve.wait_ge(s_xr[x], 16 * (j + 2))
                    dve.wait_ge(s_x1out[x], 16 * (j + 1))
                    nc.vector.tensor_tensor(x1[x][:, :], f_ps[x][:, :, :].rearrange("p k n -> p (k n)"), xr[x][:, :], ALU.add)\
                        .then_inc(s_x1[x], 1)
                    dve.wait_ge(s_x1[x], j + 2)
                    norm_measure(nc, dve, n2, x, j, x1[x][:, :])
                for x in range(2):
                    dve.wait_ge(s_turn2[x], j + 1)
                    norm_scale(nc, dve, n2, x, j, x1n[x][:, :], x1[x][:, :]).then_inc(s_x1n[x], 1)

        @block.scalar
        def _(act):
            with act.Fori(0, ROW_TILES // 2) as j:
                for x in range(2):
                    norm_root(nc, act, n1, x, j)
                for x in range(2):
                    act.wait_ge(s_turn[x], j + 2)
                    act.wait_ge(s_f[x], j + 1)
                    nc.scalar.copy(cT[x][:, :], turn_ps[x][:, :, :].rearrange("p k r -> p (k r)")).then_inc(s_cT[x], 1)
                for x in range(2):
                    norm_root(nc, act, n2, x, j)
                for x in range(2):
                    act.wait_ge(s_turn2[x], j + 2)
                    act.wait_ge(s_q[x], j + 1)
                    nc.scalar.copy(x1T[x][:, :], turn2_ps[x][:, :, :].rearrange("p k r -> p (k r)")).then_inc(s_x1T[x], 1)
                for x in range(2):
                    act.wait_ge(s_q[x], j + 2)
                    act.wait_ge(s_qout[x], 16 * (j + 1))
                    nc.scalar.copy(q_sb[x][:, :], q_ps[x][:, :, :].rearrange("p o t -> p (o t)")).then_inc(s_qsb[x], 1)

        @block.tensor
        def _(pe):
            pe.wait_ge(s_w, 16 * 5)
            pe.wait_ge(s_ones, 1)
            with pe.Fori(0, ROW_TILES // 2) as j:
                for x in range(2):
                    pe.wait_ge(s_cn[x], j + 2)
                    pe.wait_ge(s_cT[x], j + 1)
                    for k in range(KT):
                        mm = nc.tensor.transpose(turn_ps[x][:, k, :], cn[x][:, k * 128:(k + 1) * 128], ident[:, :])
                    mm.then_inc(s_turn[x], 1)
                for x in range(2):
                    pe.wait_ge(s_cT[x], j + 2)
                    pe.wait_ge(s_x1[x], j + 1)
                    dst = f_ps[x][:, :, :].rearrange("p k n -> p (k n)")
                    for k in range(KT):
                        nc.tensor.matmul(dst, cT[x][:, k * 128:(k + 1) * 128], w_f[:, k, :], start=(k == 0), stop=False)
                    nc.tensor.matmul(dst, ones[:, :], bf_row[:, :], start=False, stop=True).then_inc(s_f[x], 1)
                for x in range(2):
                    pe.wait_ge(s_x1n[x], j + 2)
                    pe.wait_ge(s_x1T[x], j + 1)
                    for k in range(KT):
                        mm = nc.tensor.transpose(turn2_ps[x][:, k, :], x1n[x][:, k * 128:(k + 1) * 128], ident[:, :])
                    mm.then_inc(s_turn2[x], 1)
                for x in range(2):
                    pe.wait_ge(s_x1T[x], j + 2)
                    pe.wait_ge(s_qsb[x], j + 1)
                    for o in range(4):
                        for k in range(KT):
                            nc.tensor.matmul(q_ps[x][:, o, :], w_q[:, k, o * 128:(o + 1) * 128], x1T[x][:, k * 128:(k + 1) * 128],
                                             start=(k == 0), stop=False)
                        mm = nc.tensor.matmul(q_ps[x][:, o, :], bq_row[:, o * 128:(o + 1) * 128], ones[:, :],
                                              start=False, stop=True)
                    mm.then_inc(s_q[x], 1)

        @block.gpsimd
        def _(pool):
            pass


def build_cope_attention(nc, n_pairs, q_heads, k_heads, v_heads, pos_emb, reach, ident_dram):
    with ExitStack() as ctx:
        sb, ps, sem, sems = allocators(nc, ctx)
        ident = sb("c_ident", [128, 128])
        emb = sb("c_emb", [D_HEAD, NPOS])
        qs = [sb(f"c_q{s}", [D_HEAD, 2, QT]) for s in range(2)]
        ks = [sb(f"c_k{s}", [D_HEAD, SEQ]) for s in range(2)]
        vs = [sb(f"c_v{s}", [128, 8, D_HEAD]) for s in range(2)]
        table = [sb(f"c_table{x}", [128, PAD]) for x in range(2)]
        gate2 = [sb(f"c_gate{x}", [128, SEQ]) for x in range(2)]
        pos = [[sb(f"c_pos{s}{x}", [128, SEQ]) for x in range(2)] for s in range(2)]
        logit = [[sb(f"c_logit{s}{x}", [128, SEQ]) for x in range(2)] for s in range(2)]
        win = [[sb(f"c_win{x}{n}", [128, 2 * SEQ]) for n in range(3)] for x in range(2)]
        base = [[sb(f"c_base{x}{l}", [128, SEQ // b]) for l, b in enumerate(LEVELS)] for x in range(2)]
        interp = [sb(f"c_interp{x}", [128, SEQ // 2, 2]) for x in range(2)]
        past1 = [sb(f"c_past1{x}", [128, SEQ // 2, 2]) for x in range(2)]
        past2 = [sb(f"c_past2{x}", [128, SEQ // 2]) for x in range(2)]
        slope = [sb(f"c_slope{x}", [128, SEQ // 2, 3]) for x in range(2)]
        bend = [sb(f"c_bend{x}", [128, SEQ // 2, 2]) for x in range(2)]
        knot = sb("c_knot", [128, 2])
        probs = [sb(f"c_probs{x}", [128, SEQ]) for x in range(2)]
        pt = sb("c_pt", [128, 8, QT])
        ones = sb("c_ones", [128, 1])
        rowmax = [sb(f"c_max{x}", [128, 1]) for x in range(2)]
        negmax = [sb(f"c_neg{x}", [128, 1]) for x in range(2)]
        den = [sb(f"c_den{x}", [128, 1]) for x in range(2)]
        rden = [sb(f"c_rden{x}", [128, 1]) for x in range(2)]
        o_sb = [sb(f"c_o{x}", [128, D_HEAD]) for x in range(2)]

        score_ps = ps("c_score_ps", [128, 2, 512])
        table_ps = ps("c_table_ps", [128, 512])
        o_ps = ps("c_o_ps", [128, 512])
        mask_ps = ps("c_mask_ps", [128, SEQ])
        pt_ps = ps("c_pt_ps", [128, 8, QT])

        s_const = sem("c_const")
        s_qk = slots(sem, "c_qk", 0)
        s_v = slots(sem, "c_v", 0)
        s_scored = sem("c_scored")
        s_tabled = sem("c_tabled")
        s_taken = sem("c_taken")
        s_scan = sem("c_scan")
        s_copy = sem("c_copy")
        s_pick = sem("c_pick")
        s_leaf = sem("c_leaf")
        s_w = sem("c_w")
        s_past = sem("c_past")
        s_start = sem("c_start")
        s_pool = sem("c_pool")
        s_read = sem("c_read")
        s_cope = sem("c_cope")
        s_z = sem("c_z")
        s_neg = sem("c_neg")
        s_exp = slots(sem, "c_exp")
        s_rden = slots(sem, "c_rden")
        s_turned = sem("c_turned")
        s_ptcopy = sem("c_ptcopy", 1)
        s_pv = sem("c_pv", 1)
        s_norm = slots(sem, "c_norm")
        s_out = dma_slots(sem, "c_out")
        s_pos, s_mask, s_base, s_base1, s_pick1, s_mask2 = (
            slots(sem, f"c_{n}", 0) for n in ("pos", "mask", "base", "base1", "pick1", "mask2"))
        s_pad = sem("c_pad")
        s_held = sem("c_held")

        block = open_block(nc, ctx, sems)
        last = n_pairs - 1

        def pairs(eng, step):
            step(0, 0)
            step(1, 1)
            with eng.Fori(1, n_pairs // 2 - 1) as j:
                step(2 * j, 0)
                step(2 * j + 1, 1)
            step(last - 1, 0)
            step(last, 1)

        def early(i, n=1):
            return isinstance(i, int) and i < n

        def bits(mask):
            return mask.bitcast(U32)

        def window(l, x):
            b = LEVELS[l]
            w = win[x][2] if l == NL - 1 else win[x][l % 2]
            return w[:, :].rearrange("p (j e) -> p j e", e=2 * b)

        @block.sync
        def _(sp):
            sp.dma_start(ident[:, :], ident_dram).then_inc(s_const, 16)
            sp.dma_start(emb[:, :], pos_emb).then_inc(s_const, 16)

            def load_queries(i, s):
                if not early(i, 2):
                    sp.wait_ge(s_scored, 2 * i - 2)
                head = i // 4
                sp.dma_start(qs[s][:, :, :], q_heads[bass.ds(head, 1), :, bass.ds((i % 4) * 2 * QT, 2 * QT)]
                             .rearrange("a d (x q) -> (a d) x q", x=2)).then_inc(s_qk[s], 16)
                sp.dma_start(ks[s][:, :], k_heads[bass.ds(head, 1)].rearrange("a d t -> (a d) t")).then_inc(s_qk[s], 16)

            def load_values(i, s):
                if not early(i, 2):
                    sp.wait_ge(s_pv, 2 * i - 1)
                sp.dma_start(vs[s][:, :, :], v_heads[bass.ds(i // 4, 1)].rearrange("a p c d -> (a p) c d")).then_inc(s_v[s], 16)

            def step(i, s):
                if not (isinstance(i, int) and i == last):
                    load_queries(i + 1, 1 - s)
                load_values(i, s)

            load_queries(0, 0)
            pairs(sp, step)

        @block.tensor
        def _(pe):
            pe.wait_ge(s_const, 32)

            def scores(i, s, x):
                g = 2 * i + x
                if x == 0:
                    pe.wait_ge(s_qk[s], 32 * (i // 2 + 1))
                if not early(g):
                    pe.wait_ge(s_taken, g)
                for n in range(2):
                    mm = nc.tensor.matmul(score_ps[:, n, :], qs[s][:, x, :], ks[s][:, n * 512:(n + 1) * 512],
                                          start=True, stop=True)
                mm = nc.tensor.matmul(table_ps[:, 0:NPOS], qs[s][:, x, :], emb[:, :], start=True, stop=True)
                mm.then_inc(s_scored, 1)

            def turn(i, s, x):
                g = 2 * i + x
                pe.wait_ge(s_exp[x], i + 2)
                pe.wait_ge(s_ptcopy, g + 1)
                for c in range(8):
                    mm = nc.tensor.transpose(pt_ps[:, c, :], probs[x][:, c * 128:(c + 1) * 128], ident[:, :])
                mm.then_inc(s_turned, 1)

            def values(i, s, x):
                g = 2 * i + x
                pe.wait_ge(s_ptcopy, g + 2)
                if x == 0:
                    pe.wait_ge(s_v[s], 16 * (i // 2 + 1))
                if x == 0 and not early(i):
                    pe.wait_ge(s_norm[0], i + 1)
                    pe.wait_ge(s_norm[1], i + 1)
                for c in range(8):
                    mm = nc.tensor.matmul(o_ps[:, x * D_HEAD:(x + 1) * D_HEAD], pt[:, c, :], vs[s][:, c, :],
                                          start=(c == 0), stop=(c == 7))
                mm.then_inc(s_pv, 1)

            def step(i, s):
                final = isinstance(i, int) and i == last
                for x in range(2):
                    if not early(i, 2):
                        turn(i - 2, s, x)
                        values(i - 2, s, x)
                    if not final:
                        scores(i + 1, 1 - s, x)

            scores(0, 0, 0)
            scores(0, 0, 1)
            pairs(pe, step)
            for i in (last - 1, last):
                for x in range(2):
                    turn(i, i % 2, x)
                    values(i, i % 2, x)

        @block.scalar
        def _(act):
            def take_gate(i, x):
                g = 2 * i + x
                act.wait_ge(s_scored, g + 1)
                if not early(i):
                    act.wait_ge(s_scan, g - 1)
                nc.scalar.activation(gate2[x][:, :], score_ps[:, :, :].rearrange("p a b -> p (a b)"), ACT.Tanh, scale=0.5 * SCALE)\
                    .then_inc(s_tabled, 1)

            def take_logits(i, s, x):
                g = 2 * i + x
                if not early(i, 2):
                    act.wait_ge(s_z, g - 3)
                nc.scalar.activation(logit[s][x][:, :], score_ps[:, :, :].rearrange("p a b -> p (a b)"), ACT.Copy, scale=SCALE)
                if not early(i):
                    act.wait_ge(s_pick, 2 * NL * (i - 1) + x + 1)
                nc.scalar.activation(table[x][:, 0:NPOS], table_ps[:, 0:NPOS], ACT.Copy).then_inc(s_taken, 1)

            def spread(i, l, x):
                at = 2 * NL * i + 2 * l + x
                if l == 0:
                    act.wait_ge(s_taken, 2 * i + x + 1)
                if not (early(i) and l == 0):
                    act.wait_ge(s_pick, at - 1)
                if l == NL - 1 and not early(i):
                    act.wait_ge(s_start, 2 * (i - 1) + x + 1)
                b = LEVELS[l]
                out = window(l, x)
                if l == 0:
                    if early(i) and x == 0:
                        act.wait_ge(s_pad, 5)
                    src = table[x][:, 0:2 * b].unsqueeze(1).to_broadcast([128, SEQ // b, 2 * b])
                    nc.scalar.activation(out, src, ACT.Copy).then_inc(s_copy, 1)
                else:
                    src = window(l - 1, x)[:, :, 0:2 * b].unsqueeze(2).to_broadcast([128, SEQ // b // 2, 2, 2 * b])
                    nc.scalar.activation(out.rearrange("p (j s) e -> p j s e", s=2), src, ACT.Copy).then_inc(s_copy, 1)

            def past(i, x):
                act.wait_ge(s_w, 2 * i + x + 1)
                nc.scalar.activation(past1[x][:, :, :], interp[x][:, :, :], ACT.Relu, bias=knot[:, 0:1])
                nc.scalar.activation(past2[x][:, :], interp[x][:, :, 1], ACT.Relu, bias=knot[:, 1:2]).then_inc(s_past, 1)

            def expo(i, x):
                g = 2 * i + x
                act.wait_ge(s_neg, g + 1)
                act.wait_ge(s_rden[x], i + 1)
                nc.scalar.activation(probs[x][:, :], probs[x][:, :], ACT.Exp, bias=negmax[x][:, :],
                                     accum_out=den[x][:, :]).then_inc(s_exp[x], 1)

            def keep(i, x):
                g = 2 * i + x
                act.wait_ge(s_turned, g + 1)
                act.wait_ge(s_pv, g + 1)
                nc.scalar.activation(pt[:, :, :], pt_ps[:, :, :], ACT.Copy).then_inc(s_ptcopy, 1)

            def norm(i, x):
                g = 2 * i + x
                act.wait_ge(s_pv, 2 * i + 3)
                act.wait_ge(s_rden[x], i + 2)
                act.wait_ge(s_out[x], 16 * (i + 1))
                nc.scalar.activation(o_sb[x][:, :], o_ps[:, x * D_HEAD:(x + 1) * D_HEAD], ACT.Copy, scale=rden[x][:, :])\
                    .then_inc(s_norm[x], 1)
                act.wait_ge(s_norm[x], i + 2)
                act.dma_start(reach(i, x), o_sb[x][:, :]).then_inc(s_out[x], 16)

            def step(i, s):
                final = isinstance(i, int) and i == last
                for l in range(NL):
                    for x in range(2):
                        spread(i, l, x)
                    if l == 0 and not early(i):
                        for x in range(2):
                            past(i - 1, x)
                    if l == 1 and not early(i, 2):
                        for x in range(2):
                            expo(i - 2, x)
                    if l in (2, 3) and not early(i, 2):
                        keep(i - 2, l - 2)
                    if l == 3 and not final:
                        take_gate(i + 1, 0)
                        take_logits(i + 1, 1 - s, 0)
                if not early(i, 2):
                    for x in range(2):
                        norm(i - 2, x)
                if not final:
                    take_gate(i + 1, 1)
                    take_logits(i + 1, 1 - s, 1)

            for x in range(2):
                take_gate(0, x)
                take_logits(0, 0, x)
            pairs(act, step)
            for x in range(2):
                past(last, x)
            for i in (last - 1, last):
                for x in range(2):
                    expo(i, x)
                for x in range(2):
                    keep(i, x)
                for x in range(2):
                    norm(i, x)
            for x in range(2):
                act.wait_ge(s_out[x], 16 * (n_pairs + 1))

        @block.vector
        def _(dve):
            nc.vector.memset(ones[:, :], 1.0).then_inc(s_pad, 1)
            for x in range(2):
                nc.vector.memset(table[x][:, NPOS:PAD], 0.0).then_inc(s_pad, 1)
            for n in range(2):
                nc.vector.memset(knot[:, n:n + 1], -1.0 - n).then_inc(s_pad, 1)
            dve.wait_ge(s_pad, 5)

            def positions(i, s, x):
                g = 2 * i + x
                dve.wait_ge(s_tabled, g + 1)
                if not early(i, 2):
                    dve.wait_ge(s_w, g - 3)
                nc.vector.tensor_tensor_scan(pos[s][x][:, :], gate2[x][:, :], ones[:, 0:1].to_broadcast([128, SEQ]), 0.0,
                                             ALU.add, ALU.add).then_inc(s_scan, 1)
                dve.wait_ge(s_scan, g + 1)
                nc.vector.tensor_scalar(pos[s][x][:, :], pos[s][x][:, :], 0.5, float(NPOS - 1), ALU.mult, ALU.min)\
                    .then_inc(s_pos[x], 1)

            def halves(l, x):
                return base[x][l][:, :].rearrange("p (j s) -> p j s", s=2)

            def starts(s, l, x):
                return pos[s][x][:, :].rearrange("p (j s b) -> p j s b", s=2, b=LEVELS[l])

            def half_mask(i, s, l, x):
                b = LEVELS[l]
                n = SEQ // b
                if l == 0 and x == 0:
                    if not early(i):
                        dve.wait_ge(s_pick1[1], (NL - 1) * i)
                elif l == 0 or (l == 1 and x == 0):
                    dve.wait_ge(s_pick, 2 * NL * i + 2 * l + x)
                elif x == 1:
                    dve.wait_ge(s_pick1[0], (NL - 1) * i + l)
                else:
                    dve.wait_ge(s_pick1[1], (NL - 1) * i + l - 1)
                if l == 0:
                    dve.wait_ge(s_pos[x], i + 1)
                    nc.vector.tensor_scalar(mask_ps[:, 0:n], pos[s][x][:, 0:SEQ:b], float(b), None, ALU.is_ge)\
                        .then_inc(s_mask[x], 1)
                else:
                    dve.wait_ge(s_base[x], (NL - 1) * i + l)
                    nc.vector.scalar_tensor_tensor(
                        out=mask_ps[:, 0:n].rearrange("p (j s) -> p j s", s=2), in0=starts(s, l, x)[:, :, :, 0], scalar=float(b),
                        in1=base[x][l - 1][:, :].unsqueeze(2).to_broadcast([128, n // 2, 2]),
                        op0=ALU.subtract, op1=ALU.is_ge).then_inc(s_mask[x], 1)

            def base1(i, l, x):
                b = LEVELS[l]
                n = SEQ // b
                if l == NL - 1 and not early(i):
                    dve.wait_ge(s_w, 2 * (i - 1) + x + 1)
                dve.wait_ge(s_mask[x], NL * i + l + 1)
                if l == 0:
                    nc.vector.tensor_scalar(base[x][0][:, :], mask_ps[:, 0:n], float(b), None, ALU.mult).then_inc(s_base[x], 1)
                else:
                    nc.vector.scalar_tensor_tensor(
                        out=halves(l, x), in0=mask_ps[:, 0:n].rearrange("p (j s) -> p j s", s=2), scalar=float(b),
                        in1=base[x][l - 1][:, :].unsqueeze(2).to_broadcast([128, n // 2, 2]),
                        op0=ALU.mult, op1=ALU.add).then_inc(s_base1[x], 1)

            def end_mask(i, s, l, x):
                b = LEVELS[l]
                dve.wait_ge(s_pick, 2 * NL * i + 2 * l + x)
                nc.vector.scalar_tensor_tensor(
                    out=mask_ps[:, 512:512 + SEQ // b // 2], in0=starts(s, l, x)[:, :, 1, 0], scalar=float(2 * b),
                    in1=base[x][l - 1][:, :], op0=ALU.subtract, op1=ALU.is_ge).then_inc(s_mask2[x], 1)

            def base2(i, l, x):
                b, at = LEVELS[l], (NL - 1) * i + l
                dve.wait_ge(s_base1[x], at)
                dve.wait_ge(s_mask2[x], at)
                nc.vector.scalar_tensor_tensor(
                    out=halves(l, x)[:, :, 1], in0=mask_ps[:, 512:512 + SEQ // b // 2], scalar=float(b), in1=halves(l, x)[:, :, 1],
                    op0=ALU.mult, op1=ALU.add).then_inc(s_leaf if l == NL - 1 else s_base[x], 1)

            def pick1(i, l, x):
                b = LEVELS[l]
                n = SEQ // b
                out = window(l, x)
                dve.wait_ge(s_mask[x], NL * i + l + 1)
                dve.wait_ge(s_copy, 2 * NL * i + 2 * l + x + 1)
                dve.sem_inc(s_held, 1)
                if l == 0:
                    nc.vector.copy_predicated(out, bits(mask_ps[:, 0:n]).unsqueeze(2).to_broadcast([128, n, 2 * b]),
                                              table[x][:, b:3 * b].unsqueeze(1).to_broadcast([128, n, 2 * b])).then_inc(s_pick, 1)
                else:
                    nc.vector.copy_predicated(
                        out.rearrange("p (j s) e -> p j s e", s=2),
                        bits(mask_ps[:, 0:n]).rearrange("p (j s) -> p j s", s=2).unsqueeze(3).to_broadcast([128, n // 2, 2, 2 * b]),
                        window(l - 1, x)[:, :, b:3 * b].unsqueeze(2).to_broadcast([128, n // 2, 2, 2 * b])).then_inc(s_pick1[x], 1)

            def pick2(i, l, x):
                b, at = LEVELS[l], (NL - 1) * i + l
                n = SEQ // b
                dve.wait_ge(s_pick1[x], at)
                dve.wait_ge(s_mask2[x], at)
                dve.sem_inc(s_held, 1)
                nc.vector.copy_predicated(
                    window(l, x).rearrange("p (j s) e -> p j s e", s=2)[:, :, 1, :],
                    bits(mask_ps[:, 512:512 + n // 2]).unsqueeze(2).to_broadcast([128, n // 2, 2 * b]),
                    window(l - 1, x)[:, :, 2 * b:4 * b]).then_inc(s_pick, 1)

            def search(i, s, l, x):
                base1(i, l, x)
                if l:
                    end_mask(i, s, l, x)
                pick1(i, l, x)
                if l:
                    base2(i, l, x)
                if x == 0:
                    half_mask(i, s, l, 1)
                elif l < NL - 1:
                    half_mask(i, s, l + 1, 0)
                if l:
                    pick2(i, l, x)

            def total(i, s, x):
                g = 2 * i + x
                dve.wait_ge(s_cope, g + 1)
                dve.wait_ge(s_taken, g + 1)
                if not early(i):
                    dve.wait_ge(s_turned, g - 1)
                dve.sem_inc(s_held, 1)
                nc.vector.tensor_tensor_reduce(probs[x][:, :], interp[x][:, :, :].rearrange("p j s -> p (j s)"), logit[s][x][:, :], 1.0, -3.0e38,
                                               ALU.add, ALU.max, rowmax[x][:, :]).then_inc(s_z, 1)
                dve.wait_ge(s_z, g + 1)
                nc.vector.tensor_scalar(negmax[x][:, :], rowmax[x][:, :], -1.0, None, ALU.mult).then_inc(s_neg, 1)

            def recip(i, x):
                g = 2 * i + x
                dve.wait_ge(s_exp[x], i + 2)
                dve.wait_ge(s_norm[x], i + 1)
                nc.vector.reciprocal(rden[x][:, :], den[x][:, :]).then_inc(s_rden[x], 1)

            def step(i, s):
                for x in range(2):
                    positions(i, s, x)
                half_mask(i, s, 0, 0)
                for l in range(NL):
                    for x in range(2):
                        search(i, s, l, x)
                    if l == 2 and not early(i):
                        total(i - 1, 1 - s, 0)
                    if l == 3 and not early(i, 2):
                        for x in range(2):
                            recip(i - 2, x)
                if not early(i):
                    total(i - 1, 1 - s, 1)

            pairs(dve, step)
            total(last, 1, 0)
            for x in range(2):
                recip(last - 1, x)
            total(last, 1, 1)
            for x in range(2):
                recip(last, x)

        @block.gpsimd
        def _(pool):
            half = [128, SEQ // 2, 2]

            def distance(i, s, x):
                g = 2 * i + x
                pool.wait_ge(s_leaf, g + 1)
                if not early(i):
                    pool.wait_ge(s_z, g - 1)
                nc.gpsimd.tensor_tensor(interp[x][:, :, :], pos[s][x][:, :].rearrange("p (j s) -> p j s", s=2),
                                        base[x][NL - 1][:, :].unsqueeze(2).to_broadcast(half), ALU.subtract).then_inc(s_w, 1)

            def bends(i, x):
                g = 2 * i + x
                v = window(NL - 1, x)
                pool.wait_ge(s_pick, 2 * NL * i + 2 * (NL - 1) + x + 1)
                nc.gpsimd.tensor_tensor(slope[x][:, :, :], v[:, :, 1:4], v[:, :, 0:3], ALU.subtract).then_inc(s_pool, 1)
                pool.wait_ge(s_pool, 6 * g + 1)
                nc.gpsimd.tensor_tensor(bend[x][:, :, :], slope[x][:, :, 1:3], slope[x][:, :, 0:2], ALU.subtract)\
                    .then_inc(s_pool, 1)

            def weigh(i, x):
                g = 2 * i + x
                v = window(NL - 1, x)
                pool.wait_ge(s_past, g + 1)
                nc.gpsimd.tensor_tensor(interp[x][:, :, :], interp[x][:, :, :], slope[x][:, :, 0:1].to_broadcast(half), ALU.mult)\
                    .then_inc(s_pool, 1)
                pool.wait_ge(s_pool, 6 * g + 3)
                nc.gpsimd.tensor_tensor(interp[x][:, :, :], interp[x][:, :, :], v[:, :, 0:1].to_broadcast(half), ALU.add)\
                    .then_inc(s_start, 1)
                nc.gpsimd.tensor_tensor(past1[x][:, :, :], past1[x][:, :, :], bend[x][:, :, 0:1].to_broadcast(half), ALU.mult)\
                    .then_inc(s_pool, 1)
                nc.gpsimd.tensor_tensor(past2[x][:, :], past2[x][:, :], bend[x][:, :, 1], ALU.mult).then_inc(s_pool, 1)
                pool.wait_ge(s_start, g + 1)
                pool.wait_ge(s_pool, 6 * g + 5)
                nc.gpsimd.tensor_tensor(interp[x][:, :, :], interp[x][:, :, :], past1[x][:, :, :], ALU.add).then_inc(s_pool, 1)
                pool.wait_ge(s_pool, 6 * g + 6)
                nc.gpsimd.tensor_tensor(interp[x][:, :, 1], interp[x][:, :, 1], past2[x][:, :], ALU.add).then_inc(s_cope, 1)

            def step(i, s):
                distance(i, s, 0)
                bends(i, 0)
                distance(i, s, 1)
                weigh(i, 0)
                bends(i, 1)
                weigh(i, 1)

            pairs(pool, step)


def build_cross_output(nc, att_rows, x1_rows, wo_t, bo, ln_g, ln_b, x2_rows, z_t, z_sums, ident_dram):
    with ExitStack() as ctx:
        sb, ps, sem, sems = allocators(nc, ctx)
        w_o = sb("r_wo", [128, KT, D])
        bo_row, ones, ident = sb("r_bo", [1, D]), sb("r_ones", [1, 128]), sb("r_ident", [128, 128])
        gain, shift = sb("r_gain", [128, D]), sb("r_shift", [128, D])
        att, aT, x1, x2, y, z, zT = ([sb(f"r_{n}{x}", [128, D]) for x in range(2)] for n in (
            "att", "aT", "x1", "x2", "y", "z", "zT"))
        zsum = sb("r_zsum", [128, D])
        turn_ps, f_ps, turn2_ps = ([ps(f"r_{n}{x}", [128, KT, 128]) for x in range(2)] for n in ("tps", "fps", "t2ps"))
        s_w, s_ones = sem("r_w"), sem("r_ones")
        s_turn, s_aT, s_f, s_x2, s_y, s_zn, s_zg, s_z, s_added, s_turn2, s_zT = (
            slots(sem, f"r_s{n}") for n in ("turn", "aT", "f", "x2", "y", "zn", "zg", "z", "added", "turn2", "zT"))
        s_att, s_x1, s_x2out, s_zout = (dma_slots(sem, f"r_s{n}") for n in ("att", "x1", "x2out", "zout"))
        s_zero, s_sumout = sem("r_zero"), sem("r_sumout", 16)
        n1, n2 = norm_buffers(sb, sem, "r_n1"), norm_buffers(sb, sem, "r_n2")
        block = open_block(nc, ctx, sems)
        PER = ROW_TILES // B // 2

        @block.sync
        def _(sp):
            sp.dma_start(ident[:, :], ident_dram).then_inc(s_w, 16)
            sp.dma_start(w_o[:, :, :], wo_t.rearrange("(k p) n -> p k n", p=128)).then_inc(s_w, 16)
            sp.dma_start(bo_row[:, :], bo.rearrange("(a n) -> a n", a=1)).then_inc(s_w, 16)
            for dst, a in ((gain, ln_g), (shift, ln_b)):
                sp.dma_start(dst[:, :], a.rearrange("(a n) -> a n", a=1).to_broadcast([128, D])).then_inc(s_w, 16)
            with sp.Fori(0, B) as b:
                with sp.Fori(0, PER) as jj:
                    j = b * PER + jj
                    for x in range(2):
                        sp.wait_ge(s_turn[x], j + 1)
                        sp.dma_start(att[x][:, :], row_tile(att_rows, j, x)).then_inc(s_att[x], 16)
                        sp.wait_ge(s_x2[x], j + 1)
                        sp.dma_start(x1[x][:, :], row_tile(x1_rows, j, x)).then_inc(s_x1[x], 16)
                    for x in range(2):
                        sp.wait_ge(s_x2[x], j + 2)
                        sp.dma_start(row_tile(x2_rows, j, x), x2[x][:, :]).then_inc(s_x2out[x], 16)
                    for x in range(2):
                        sp.wait_ge(s_zT[x], j + 2)
                        dst = z_t[bass.ds(b, 1), :, bass.ds((2 * jj + x) * 128, 128)]
                        sp.dma_start(dst.rearrange("a (k p) t -> (a p) k t", p=128),
                                     zT[x][:, :].rearrange("p (k t) -> p k t", k=KT)).then_inc(s_zout[x], 16)
                sp.wait_ge(s_added[1], (b + 1) * PER + 1)
                sp.dma_start(z_sums[bass.ds(b, 1)].rearrange("a p n -> (a p) n"), zsum[:, :]).then_inc(s_sumout, 16)
            for s in (s_x2out, s_zout):
                for x in range(2):
                    sp.wait_ge(s[x], 16 * (ROW_TILES // 2 + 1))
            sp.wait_ge(s_sumout, 16 * (B + 1))

        @block.vector
        def _(dve):
            nc.vector.memset(ones[:, :], 1.0).then_inc(s_ones, 1)
            dve.wait_ge(s_w, 16 * 5)
            with dve.Fori(0, B) as b:
                dve.wait_ge(s_sumout, 16 * (b + 1))
                nc.vector.memset(zsum[:, :], 0.0).then_inc(s_zero, 1)
                with dve.Fori(0, PER) as jj:
                    j = b * PER + jj
                    for x in range(2):
                        dve.wait_ge(s_f[x], j + 2)
                        dve.wait_ge(s_x1[x], 16 * (j + 2))
                        dve.wait_ge(s_x2out[x], 16 * (j + 1))
                        nc.vector.tensor_tensor(x2[x][:, :], f_ps[x][:, :, :].rearrange("p k n -> p (k n)"), x1[x][:, :], ALU.add)\
                            .then_inc(s_x2[x], 1)
                        dve.wait_ge(s_x2[x], j + 2)
                        norm_measure(nc, dve, n1, x, j, x2[x][:, :])
                    for x in range(2):
                        norm_scale(nc, dve, n1, x, j, y[x][:, :], x2[x][:, :]).then_inc(s_y[x], 1)
                        dve.wait_ge(s_y[x], j + 2)
                        norm_measure(nc, dve, n2, x, j, y[x][:, :])
                    for x in range(2):
                        norm_scale(nc, dve, n2, x, j, y[x][:, :], y[x][:, :]).then_inc(s_zn[x], 1)
                        dve.wait_ge(s_zn[x], j + 2)
                        nc.vector.tensor_tensor(y[x][:, :], y[x][:, :], gain[:, :], ALU.mult).then_inc(s_zg[x], 1)
                        dve.wait_ge(s_zg[x], j + 2)
                        dve.wait_ge(s_turn2[x], j + 1)
                        nc.vector.tensor_tensor(z[x][:, :], y[x][:, :], shift[:, :], ALU.add).then_inc(s_z[x], 1)
                        dve.wait_ge(s_z[x], j + 2)
                        if x:
                            dve.wait_ge(s_added[0], j + 2)
                        else:
                            dve.wait_ge(s_added[1], j + 1)
                            dve.wait_ge(s_zero, b + 1)
                        nc.vector.tensor_tensor(zsum[:, :], zsum[:, :], z[x][:, :], ALU.add).then_inc(s_added[x], 1)

        @block.scalar
        def _(act):
            with act.Fori(0, ROW_TILES // 2) as j:
                for x in range(2):
                    act.wait_ge(s_turn[x], j + 2)
                    act.wait_ge(s_f[x], j + 1)
                    nc.scalar.copy(aT[x][:, :], turn_ps[x][:, :, :].rearrange("p k r -> p (k r)")).then_inc(s_aT[x], 1)
                for n in (n1, n2):
                    for x in range(2):
                        norm_root(nc, act, n, x, j)
                for x in range(2):
                    act.wait_ge(s_turn2[x], j + 2)
                    act.wait_ge(s_zout[x], 16 * (j + 1))
                    nc.scalar.copy(zT[x][:, :], turn2_ps[x][:, :, :].rearrange("p k r -> p (k r)")).then_inc(s_zT[x], 1)

        @block.tensor
        def _(pe):
            pe.wait_ge(s_w, 16 * 5)
            pe.wait_ge(s_ones, 1)
            with pe.Fori(0, ROW_TILES // 2) as j:
                for x in range(2):
                    pe.wait_ge(s_att[x], 16 * (j + 2))
                    pe.wait_ge(s_aT[x], j + 1)
                    for k in range(KT):
                        mm = nc.tensor.transpose(turn_ps[x][:, k, :], att[x][:, k * 128:(k + 1) * 128], ident[:, :])
                    mm.then_inc(s_turn[x], 1)
                for x in range(2):
                    pe.wait_ge(s_aT[x], j + 2)
                    pe.wait_ge(s_x2[x], j + 1)
                    dst = f_ps[x][:, :, :].rearrange("p k n -> p (k n)")
                    for k in range(KT):
                        nc.tensor.matmul(dst, aT[x][:, k * 128:(k + 1) * 128], w_o[:, k, :], start=(k == 0), stop=False)
                    nc.tensor.matmul(dst, ones[:, :], bo_row[:, :], start=False, stop=True).then_inc(s_f[x], 1)
                for x in range(2):
                    pe.wait_ge(s_z[x], j + 2)
                    pe.wait_ge(s_zT[x], j + 1)
                    for k in range(KT):
                        mm = nc.tensor.transpose(turn2_ps[x][:, k, :], z[x][:, k * 128:(k + 1) * 128], ident[:, :])
                    mm.then_inc(s_turn2[x], 1)

        @block.gpsimd
        def _(pool):
            pass


def build_experts(nc, z_sums, bn_g, bn_b, bn_mean, bn_var, wr, br, w_down, b_down, w_up, b_up, z_t, x2_rows, out_rows, ident_dram):
    with ExitStack() as ctx:
        sb, ps, sem, sems = allocators(nc, ctx)
        ident = sb("e_ident", [128, 128])
        zs = sb("e_zs", [128, B, D])
        ones = sb("e_ones", [128, 128])
        cols = sb("e_cols", [128, 4, KT])
        wr_sb, br_row = sb("e_wr", [128, KT, E]), sb("e_br", [1, E])
        wd = sb("e_wd", [128, KT, E, H])
        wu, bd, bu = sb("e_wu", [H, E, D]), sb("e_bd", [H, E]), sb("e_bu", [E, D])
        rstd, mean_col, norm_col = sb("e_rstd", [128, KT]), sb("e_mean", [128, KT, B]), sb("e_norm", [128, KT, B])
        logits, mx, negmx, ex, total, pick = (sb(f"e_{n}", [B, m]) for n, m in (
            ("logits", E), ("mx", 1), ("negmx", 1), ("ex", E), ("total", 1), ("pick", 2 * E + 1)))
        order, first = sb("e_order", [B, E]), sb("e_first", [B, 1])
        placed = sb("e_placed", [B, B, E + 1])
        chosen = sb("e_chosen", [128, B, E + 1])
        row_pick = sb("e_rowpick", [E, B, 128])
        wd_b = [sb(f"e_wdb{b}", [128, KT, H]) for b in range(B)]
        wu_b = [sb(f"e_wub{b}", [H, D]) for b in range(B)]
        bd_b, tmp = sb("e_bdb", [H, B]), sb("e_tmp", [H, E])
        zt = [sb(f"e_zt{n}", [128, KT, 512]) for n in range(2)]
        h_sb = [sb(f"e_h{n}", [H, 512]) for n in range(2)]
        xr = [sb(f"e_xr{n}", [128, 4, D]) for n in range(2)]
        mean_ps, misc_ps = ps("e_meanps", [128, 512]), ps("e_miscps", [128, 512])
        h_ps = [ps(f"e_hps{n}", [128, 512]) for n in range(2)]
        y_ps = [ps(f"e_yps{n}", [128, 512]) for n in range(4)]
        s_in, s_ones, s_mean, s_dve, s_pe, s_act, s_order = (sem(f"e_s{n}") for n in ("in", "ones", "mean", "dve", "pe", "act", "order"))
        s_zt, s_xr, s_h, s_hsb, s_out = (slots(sem, f"e_s{n}", 0) for n in ("zt", "xr", "h", "hsb", "out"))
        s_y = [sem(f"e_sy{n}") for n in range(4)]
        s_ysb = [sem(f"e_sysb{n}") for n in range(4)]
        block = open_block(nc, ctx, sems)
        HALVES = SEQ // 512

        @block.sync
        def _(sp):
            one = lambda a: a.rearrange("(a n) -> a n", a=1)
            with nc.allow_non_contiguous_dma(reason="vectors of 512 as columns"):
                loads = [(ident[:, :], ident_dram), (zs[:, :, :], z_sums.rearrange("b p n -> p b n")),
                         (wr_sb[:, :, :], wr.rearrange("(k p) e -> p k e", p=128)), (br_row[:, :], one(br)),
                         (wu[:, :, :], w_up.rearrange("e h n -> h e n")), (bu[:, :], b_up),
                         (bd[:, :], b_down.rearrange("e h -> h e"))]
                loads += [(cols[:, n, :], a.rearrange("(k p) -> p k", p=128)) for n, a in enumerate((bn_g, bn_b, bn_mean, bn_var))]
                loads += [(wd[:, k, :, :], w_down[:, k * 128:(k + 1) * 128, :].rearrange("e p h -> p e h")) for k in range(KT)]
                for dst, src in loads:
                    sp.dma_start(dst, src).then_inc(s_in, 16)
                assert len(loads) == N_LOADS
            for b in range(B):
                for n in range(HALVES):
                    sp.wait_ge(s_h[n], b)
                    sp.dma_start(zt[n][:, :, :], z_t[b, :, n * 512:(n + 1) * 512].rearrange("(k p) t -> p k t", p=128))\
                        .then_inc(s_zt[n], 16)
                    sp.wait_ge(s_out[n], 16 * b)
                    at = b * SEQ + n * 512
                    sp.dma_start(xr[n][:, :, :], x2_rows[at:at + 512, :].rearrange("(c p) n -> p c n", p=128))\
                        .then_inc(s_xr[n], 16)
                for n in range(HALVES):
                    at = b * SEQ + n * 512
                    for c in range(4):
                        sp.wait_ge(s_ysb[c], 2 * b + n + 1)
                    sp.dma_start(out_rows[at:at + 512, :].rearrange("(c p) n -> p c n", p=128), xr[n][:, :, :])\
                        .then_inc(s_out[n], 16)
            for n in range(HALVES):
                sp.wait_ge(s_out[n], 16 * B)

        @block.gpsimd
        def _(pool):
            nc.gpsimd.iota(order[:, :], pattern=[[-1, E]], base=E, channel_multiplier=0,
                           allow_small_or_imprecise_dtypes=True).then_inc(s_order, 1)

        steps = {}

        @block.vector
        def _(dve):
            done = [0]

            def finished(name=None):
                done[0] += 1
                if name:
                    steps[name] = done[0]
                dve.wait_ge(s_dve, done[0])

            nc.vector.memset(ones[:, :], 1.0).then_inc(s_ones, 1)
            dve.wait_ge(s_in, 16 * N_LOADS)
            nc.vector.tensor_scalar(rstd[:, :], cols[:, 3, :], EPS, None, ALU.add).then_inc(s_dve, 1)
            finished("var")
            dve.wait_ge(s_act, 1)
            nc.vector.reciprocal(rstd[:, :], rstd[:, :]).then_inc(s_dve, 1)
            finished()
            nc.vector.tensor_tensor(rstd[:, :], rstd[:, :], cols[:, 0, :], ALU.mult).then_inc(s_dve, 1)
            finished()
            dve.wait_ge(s_pe, 1)
            nc.vector.tensor_scalar(mean_col[:, :, :], mean_ps[:, 0:KT * B].rearrange("p (k b) -> p k b", b=B),
                                        1.0 / SEQ, None, ALU.mult).then_inc(s_dve, 1)
            finished()
            for k in range(KT):
                nc.vector.tensor_scalar(norm_col[:, k, :], mean_col[:, k, :], cols[:, 2, k:k + 1], rstd[:, k:k + 1],
                                            ALU.subtract, ALU.mult).then_inc(s_dve, 1)
                finished()
                nc.vector.tensor_scalar(norm_col[:, k, :], norm_col[:, k, :], cols[:, 1, k:k + 1], None, ALU.add).then_inc(s_dve, 1)
                finished("norm")
            dve.wait_ge(s_pe, 2)
            nc.vector.tensor_copy(logits[:, :], misc_ps[0:B, 0:E]).then_inc(s_dve, 1)
            finished()
            nc.vector.tensor_reduce(mx[:, :], logits[:, :], AX.X, ALU.max).then_inc(s_dve, 1)
            finished()
            nc.vector.tensor_scalar(negmx[:, :], mx[:, :], -1.0, None, ALU.mult).then_inc(s_dve, 1)
            finished("negmx")
            dve.wait_ge(s_order, 1)
            nc.vector.tensor_scalar(pick[:, 0:E], logits[:, :], mx[:, 0:1], None, ALU.is_equal).then_inc(s_dve, 1)
            finished()
            nc.vector.tensor_tensor(pick[:, 0:E], pick[:, 0:E], order[:, :], ALU.mult).then_inc(s_dve, 1)
            finished()
            nc.vector.tensor_reduce(first[:, :], pick[:, 0:E], AX.X, ALU.max).then_inc(s_dve, 1)
            finished()
            nc.vector.tensor_scalar(pick[:, E:2 * E], order[:, :], first[:, 0:1], None, ALU.is_equal).then_inc(s_dve, 1)
            finished()
            dve.wait_ge(s_act, 2)
            nc.vector.reciprocal(pick[:, 2 * E:2 * E + 1], total[:, :]).then_inc(s_dve, 1)
            finished()
            for b in range(B):
                nc.vector.tensor_scalar(placed[:, b, :], pick[:, E:2 * E + 1], ident[0:B, b:b + 1], None, ALU.mult).then_inc(s_dve, 1)
                finished("placed")
            dve.wait_ge(s_pe, 3)
            nc.vector.tensor_copy(chosen[:, :, :], misc_ps[:, 64:64 + B * (E + 1)].rearrange("p (b e) -> p b e", b=B)).then_inc(s_dve, 1)
            finished()
            nc.vector.tensor_copy(row_pick[:, :, :], mean_ps[0:E, 0:512].rearrange("e (b t) -> e b t", b=B)).then_inc(s_dve, 1)
            finished("rowpick")
            for b in range(B):
                for e in range(E):
                    if e == 0:
                        nc.vector.tensor_scalar(wd_b[b][:, :, :], wd[:, :, e, :], chosen[:, b, e:e + 1], None, ALU.mult).then_inc(s_dve, 1)
                        finished()
                        nc.vector.tensor_scalar(wu_b[b][:, :], wu[:, e, :], chosen[0:H, b, e:e + 1], None, ALU.mult).then_inc(s_dve, 1)
                        finished()
                    else:
                        nc.vector.scalar_tensor_tensor(out=wd_b[b][:, :, :], in0=wd[:, :, e, :], scalar=chosen[:, b, e:e + 1],
                                                           in1=wd_b[b][:, :, :], op0=ALU.mult, op1=ALU.add).then_inc(s_dve, 1)
                        finished()
                        nc.vector.scalar_tensor_tensor(out=wu_b[b][:, :], in0=wu[:, e, :], scalar=chosen[0:H, b, e:e + 1],
                                                           in1=wu_b[b][:, :], op0=ALU.mult, op1=ALU.add).then_inc(s_dve, 1)
                        finished()
                nc.vector.tensor_tensor(tmp[:, :], bd[:, :], chosen[0:H, b, 0:E], ALU.mult).then_inc(s_dve, 1)
                finished()
                nc.vector.tensor_reduce(bd_b[:, b:b + 1], tmp[:, :], AX.X, ALU.add).then_inc(s_dve, 1)
                finished(f"weights{b}")
                for n in range(HALVES):
                    dve.wait_ge(s_xr[n], 16 * (b + 1))
                    for c in range(4):
                        dve.wait_ge(s_y[c], 2 * b + n + 1)
                        nc.vector.scalar_tensor_tensor(out=xr[n][:, c, :], in0=y_ps[c][:, :], scalar=chosen[:, b, E:E + 1],
                                                       in1=xr[n][:, c, :], op0=ALU.mult, op1=ALU.add).then_inc(s_ysb[c], 1)

        @block.scalar
        def _(act):
            act.wait_ge(s_dve, steps["var"])
            nc.scalar.activation(rstd[:, :], rstd[:, :], ACT.Sqrt).then_inc(s_act, 1)
            act.wait_ge(s_dve, steps["negmx"])
            nc.scalar.activation(ex[:, :], logits[:, :], ACT.Exp, bias=negmx[:, :], accum_out=total[:, :]).then_inc(s_act, 1)
            for b in range(B):
                act.wait_ge(s_dve, steps[f"weights{b}"])
                for n in range(HALVES):
                    act.wait_ge(s_h[n], b + 1)
                    if b:
                        act.wait_ge(s_y[3], 2 * (b - 1) + n + 1)
                    nc.scalar.activation(h_sb[n][:, :], h_ps[n][0:H, :], ACT.Relu, bias=bd_b[:, b:b + 1]).then_inc(s_hsb[n], 1)

        @block.tensor
        def _(pe):
            pe.wait_ge(s_in, 16 * N_LOADS)
            pe.wait_ge(s_ones, 1)
            for k in range(KT):
                for b in range(B):
                    mm = nc.tensor.matmul(mean_ps[:, k * B + b:k * B + b + 1], zs[:, b, k * 128:(k + 1) * 128], ones[:, 0:1],
                                          start=True, stop=True)
            mm.then_inc(s_pe, 1)
            pe.wait_ge(s_dve, steps["norm"])
            for k in range(KT):
                nc.tensor.matmul(misc_ps[0:B, 0:E], norm_col[:, k, :], wr_sb[:, k, :], start=(k == 0), stop=False)
            nc.tensor.matmul(misc_ps[0:B, 0:E], ones[0:1, 0:B], br_row[:, :], start=False, stop=True).then_inc(s_pe, 1)
            pe.wait_ge(s_dve, steps["placed"])
            for b in range(B):
                nc.tensor.matmul(mean_ps[0:E, b * 128:(b + 1) * 128], placed[:, b, 0:E], ones[0:B, :], start=True, stop=True)
            nc.tensor.matmul(misc_ps[:, 64:64 + B * (E + 1)], ones[0:B, :], placed[:, :, :].rearrange("p b e -> p (b e)"),
                             start=True, stop=True).then_inc(s_pe, 1)
            pe.wait_ge(s_dve, steps["rowpick"])
            for b in range(B):
                pe.wait_ge(s_dve, steps[f"weights{b}"])
                for n in range(HALVES):
                    pe.wait_ge(s_zt[n], 16 * (b + 1))
                    pe.wait_ge(s_hsb[n], b)
                    for k in range(KT):
                        mm = nc.tensor.matmul(h_ps[n][0:H, :], wd_b[b][:, k, :], zt[n][:, k, :], start=(k == 0), stop=(k == KT - 1))
                    mm.then_inc(s_h[n], 1)
                for n in range(HALVES):
                    pe.wait_ge(s_hsb[n], b + 1)
                    for c in range(4):
                        pe.wait_ge(s_ysb[c], 2 * b + n)
                        nc.tensor.matmul(y_ps[c][:, :], h_sb[n][:, c * 128:(c + 1) * 128], wu_b[b][:, :], start=True, stop=False)
                        nc.tensor.matmul(y_ps[c][:, :], row_pick[:, b, :], bu[:, :], start=False, stop=True).then_inc(s_y[c], 1)


def build_decoder_layer(nc, a):
    def scratch(name, shape):
        return nc.dram_tensor(name, shape, F32).ap()

    xn_rows, ctx_rows, x1_rows, att_rows, x2_rows = (scratch(f"t_{n}", [ROWS, D]) for n in ("xn", "ctx", "x1", "att", "x2"))
    qa, ka = scratch("t_qa", [A_HEADS, DH, SEQ]), scratch("t_ka", [A_HEADS, DH, SEQ])
    va, vb = scratch("t_va", [A_HEADS, 128, 8, DH]), scratch("t_vb", [B * HEADS, 128, 8, DH])
    qb, kb = scratch("t_qb", [B, D, SEQ]), scratch("t_kb", [B, D, SEQ])
    z_t, z_sums = scratch("t_zt", [B, D, SEQ]), scratch("t_zsums", [B, 128, D])
    x_rows, out_rows, ident = a["x"].rearrange("b s d -> (b s) d"), a["out"].rearrange("b s d -> (b s) d"), a["ident"]

    def self_place(i, x, half):
        row = (i // 4) * 64
        col = ((i % 4) * 2 + x) * 2 * DH + half * DH
        return ctx_rows[bass.ds(row, 64), bass.ds(col, DH)]

    def cross_place(i, x):
        head = i // 4
        row = (head // HEADS) * SEQ + ((i % 4) * 2 + x) * QT
        return att_rows[bass.ds(row, QT), bass.ds((head % HEADS) * DH, DH)]

    build_memory_projections(nc, a["ctx_t"], a["xwk"], a["xbk"], a["xwv"], a["xbv"], kb, vb)
    build_self_projections(nc, x_rows, a["wq"], a["bq"], a["wk"], a["bk"], a["wv"], a["bv"], xn_rows, qa, ka, va, ident)
    build_self_attention(nc, qa, ka, va, self_place, ident)
    build_self_output(nc, ctx_rows, xn_rows, x_rows, a["wf"], a["bf"], a["xwq"], a["xbq"], x1_rows, qb, ident)
    build_cope_attention(nc, B * HEADS * 4, qb.rearrange("b (h d) t -> (b h) d t", d=DH),
                         kb.rearrange("b (h d) t -> (b h) d t", d=DH), vb, a["emb"], cross_place, ident)
    build_cross_output(nc, att_rows, x1_rows, a["xwo"], a["xbo"], a["ln_g"], a["ln_b"], x2_rows, z_t, z_sums, ident)
    build_experts(nc, z_sums, a["bn_g"], a["bn_b"], a["bn_mean"], a["bn_var"], a["wr"], a["br"], a["w_down"], a["b_down"],
                  a["w_up"], a["b_up"], z_t, x2_rows, out_rows, ident)


def lay_out(inputs):
    import numpy as np

    n = {k: np.asarray(v) for k, v in inputs.items()}
    attn, xattn, ffn = (lambda k, p=p: n[f"L0_{p}_{k}"] for p in ("attn", "xattn", "ffn"))
    evens = [g * DH + d for par in range(2) for g in range(par, HEADS, 2) for d in range(DH)]
    arrays = {
        "x": n["x"], "ctx_t": n["ctx_1024"][:, ::-1, :].transpose(0, 2, 1),
        "wq": attn("Wq"), "bq": attn("bq"), "wk": attn("Wk"), "bk": attn("bk"),
        "wv": attn("Wv")[:, evens], "bv": attn("bv")[evens], "wf": attn("Wf"), "bf": attn("bf"),
        "xwq": xattn("Wq_w").T, "xbq": xattn("Wq_b"), "xwk": xattn("Wk_w").T, "xbk": xattn("Wk_b"),
        "xwv": xattn("Wv_w").T, "xbv": xattn("Wv_b"), "xwo": xattn("Wo_w").T, "xbo": xattn("Wo_b"),
        "emb": xattn("pos_emb"),
        "ln_g": ffn("ln_g"), "ln_b": ffn("ln_b"), "bn_g": ffn("bn_g"), "bn_b": ffn("bn_b"),
        "bn_mean": ffn("bn_mean"), "bn_var": ffn("bn_var"), "wr": ffn("Wr"), "br": ffn("br"),
        "w_down": ffn("W_down"), "b_down": ffn("b_down"), "w_up": ffn("W_up"), "b_up": ffn("b_up"),
        "ident": np.eye(128, dtype=np.float32),
    }
    return {k: np.ascontiguousarray(v) for k, v in arrays.items()}


def kernel(**inputs):
    import concourse.bacc as bacc
    from concourse.bass_utils import run_bass_kernel_spmd

    nc = bacc.Bacc("TRN2", target_bir_lowering=False, num_devices=1)
    given = lay_out(inputs)
    arrays = {f"in_{k}": v for k, v in given.items()}
    aps = {k: nc.dram_tensor(f"in_{k}", v.shape, mybir.dt.from_np(v.dtype), kind="ExternalInput").ap() for k, v in given.items()}
    aps["out"] = nc.dram_tensor("out_0", (B, SEQ, D), F32, kind="ExternalOutput").ap()
    build_decoder_layer(nc, aps)
    r = run_bass_kernel_spmd(nc, [arrays], core_ids=[0])
    return r.results[0]["out_0"]
```
